# Optimizing a Trainium2 kernel written in Bass

```python
import numpy as np
import jax
import jax.numpy as jnp

def _softmax(x, axis=-1):
    return jax.nn.softmax(x, axis=axis)

def _gelu(x):
    return jax.nn.gelu(x, approximate=True)

def _silu(x):
    return jax.nn.silu(x)

def _sigmoid(x):
    return jax.nn.sigmoid(x)

def _layernorm(x, axis=-1, eps=1e-05):
    m = jnp.mean(x, axis=axis, keepdims=True)
    v = jnp.var(x, axis=axis, keepdims=True)
    return (x - m) / jnp.sqrt(v + eps)

def _scatter_add(tgt, idx, src, axis=0):
    return tgt.at[idx].add(src)

def _segment_sum(src, seg, n):
    return jax.ops.segment_sum(src, seg, n)
kernel_name = 'mk_xattn_ffn_d1_seqx_r4_b57ee9'

def setup_inputs(seed: int=0):
    np.random.seed(seed)
    _w = jnp.asarray

    def _rec_inputs():
        import jax
        import jax.numpy as jnp
        _rk = jax.random.key(seed)
        x = -0.0002928 + 1 * jax.random.normal(jax.random.fold_in(_rk, 1), (32, 256, 256), jnp.float32)
        _lenS = 256 - jax.random.randint(jax.random.fold_in(_rk, 7), (32,), 0, max(1, 256 // 4) + 1, jnp.int32)
        _lenS2 = 256 - jax.random.randint(jax.random.fold_in(_rk, 8), (32,), 0, max(1, 256 // 4) + 1, jnp.int32)
        _ctx_1024P = jax.random.normal(jax.random.fold_in(_rk, 11), (32, 16, 256), jnp.float32)
        _ctx_1024c = jax.random.dirichlet(jax.random.fold_in(_rk, 511), 0.3 * jnp.ones((16,), jnp.float32), (32, 256))
        _ctx_1024t = jnp.einsum('bsk,bkd->bsd', _ctx_1024c, _ctx_1024P)
        _ctx_1024t = _ctx_1024t * jax.lax.rsqrt(jnp.mean(jnp.square(_ctx_1024t)) + 1e-12) * 0.953939
        ctx_1024 = -1.39393e-06 + 0.999914 * (_ctx_1024t + 0.3 * jax.random.normal(jax.random.fold_in(_rk, 611), (32, 256, 256), jnp.float32))
        fside_Bx1xSxS2_0 = -4.48278e-06 + 1.00019 * jax.random.normal(jax.random.fold_in(_rk, 12), (32, 1, 256, 256), jnp.float32)
        return (x, ctx_1024, fside_Bx1xSxS2_0)
    x, ctx_1024, fside_Bx1xSxS2_0 = _rec_inputs()

    def _L0_xattn_setup():
        import jax, jax.numpy as jnp
        import numpy as np
        B, S, D_FF = (2, 512, 256)
        NUM_HEADS, D_KV = (16, 64)
        INNER = NUM_HEADS * D_KV
        key = jax.random.key(seed)
        ks = jax.random.split(key, 8)
        scale = 1.0 / np.sqrt(D_FF)
        return {'q': jax.random.normal(ks[0], (B, S, D_FF), jnp.float32), 'k': jax.random.normal(ks[1], (B, S, D_FF), jnp.float32), 'v': jax.random.normal(ks[2], (B, S, D_FF), jnp.float32), 'attn_mask': jax.random.normal(ks[3], (B, 1, S, S), jnp.float32), 'Wq': jax.random.normal(ks[4], (INNER, D_FF), jnp.float32) * scale, 'Wk': jax.random.normal(ks[5], (INNER, D_FF), jnp.float32) * scale, 'Wv': jax.random.normal(ks[6], (INNER, D_FF), jnp.float32) * scale, 'Wo': jax.random.normal(ks[7], (D_FF, INNER), jnp.float32) * scale, 'num_heads': NUM_HEADS}
    _L0_xattn_all = _L0_xattn_setup()
    _L0_xattn_in = {k: v for k, v in _L0_xattn_all.items() if k in ('Wq', 'Wk', 'Wv', 'Wo')}
    del _L0_xattn_all

    def _L0_ffn_setup():
        import jax, jax.numpy as jnp
        import numpy as np
        from jax import lax
        DIM = 256
        INTER = 128
        N_EXPERTS = 16
        TOPK = 4
        ROUTE_SCALE = 2.5
        VOCAB = 8000

        def _silu_and_mul(gu):
            gate, up = jnp.split(gu, 2, axis=-1)
            return jax.nn.silu(gate) * up
        key = jax.random.key(seed)
        ks = jax.random.split(key, 8)
        x = jax.random.normal(ks[0], (2, 128, DIM), dtype=jnp.float32)
        input_ids = jax.random.randint(ks[1], (2, 128), 0, VOCAB)
        s = 0.02
        gate_w = jax.random.normal(ks[2], (N_EXPERTS, DIM), dtype=jnp.float32) * s
        gate_b = jax.random.normal(ks[3], (N_EXPERTS,), dtype=jnp.float32) * s
        w13 = jax.random.normal(ks[4], (N_EXPERTS, 2 * INTER, DIM), dtype=jnp.float32) * s
        w2 = jax.random.normal(ks[5], (N_EXPERTS, DIM, INTER), dtype=jnp.float32) * s
        w13_s = jax.random.normal(ks[6], (2 * INTER, DIM), dtype=jnp.float32) * s
        w2_s = jax.random.normal(ks[7], (DIM, INTER), dtype=jnp.float32) * s
        return {'x': x, 'input_ids': input_ids, 'gate_w': gate_w, 'gate_b': gate_b, 'w13': w13, 'w2': w2, 'w13_s': w13_s, 'w2_s': w2_s}
    _L0_ffn_all = _L0_ffn_setup()
    _L0_ffn_in = {k: v for k, v in _L0_ffn_all.items() if k in ('input_ids', 'gate_w', 'gate_b', 'w13', 'w2', 'w13_s', 'w2_s')}
    del _L0_ffn_all
    return {'x': x, 'ctx_1024': ctx_1024, 'fside_Bx1xSxS2_0': fside_Bx1xSxS2_0, 'L0_xattn_Wq': _L0_xattn_in['Wq'], 'L0_xattn_Wk': _L0_xattn_in['Wk'], 'L0_xattn_Wv': _L0_xattn_in['Wv'], 'L0_xattn_Wo': _L0_xattn_in['Wo'], 'L0_ffn_input_ids': _L0_ffn_in['input_ids'], 'L0_ffn_gate_w': _L0_ffn_in['gate_w'], 'L0_ffn_gate_b': _L0_ffn_in['gate_b'], 'L0_ffn_w13': _L0_ffn_in['w13'], 'L0_ffn_w2': _L0_ffn_in['w2'], 'L0_ffn_w13_s': _L0_ffn_in['w13_s'], 'L0_ffn_w2_s': _L0_ffn_in['w2_s']}

def reference(x, ctx_1024, fside_Bx1xSxS2_0, L0_xattn_Wq, L0_xattn_Wk, L0_xattn_Wv, L0_xattn_Wo, L0_ffn_input_ids, L0_ffn_gate_w, L0_ffn_gate_b, L0_ffn_w13, L0_ffn_w2, L0_ffn_w13_s, L0_ffn_w2_s):
    import jax
    import jax.numpy as jnp

    def _L0_xattn_ref(q, k, v, attn_mask, Wq, Wk, Wv, Wo, num_heads):
        import jax, jax.numpy as jnp
        import numpy as np
        B, S, D_FF = (2, 512, 256)
        NUM_HEADS, D_KV = (16, 64)
        INNER = NUM_HEADS * D_KV
        b, s, _ = q.shape

        def proj_heads(x, W):
            y = jnp.einsum('bsd,ed->bse', x, W)
            return y.reshape(b, s, num_heads, -1).transpose(0, 2, 1, 3)
        qh = proj_heads(q, Wq)
        kh = proj_heads(k, Wk)
        vh = proj_heads(v, Wv)
        scores = jnp.einsum('bhqd,bhkd->bhqk', qh, kh) + attn_mask
        probs = jax.nn.softmax(scores, axis=-1)
        ctx = jnp.einsum('bhqk,bhkd->bhqd', probs, vh)
        ctx = ctx.transpose(0, 2, 1, 3).reshape(b, s, -1)
        return jnp.einsum('bse,de->bsd', ctx, Wo)

    def _L0_ffn_ref(x, input_ids, gate_w, gate_b, w13, w2, w13_s, w2_s):
        import jax, jax.numpy as jnp
        import numpy as np
        from jax import lax
        DIM = 256
        INTER = 128
        N_EXPERTS = 16
        TOPK = 4
        ROUTE_SCALE = 2.5
        VOCAB = 8000

        def _silu_and_mul(gu):
            gate, up = jnp.split(gu, 2, axis=-1)
            return jax.nn.silu(gate) * up
        B, S, D = x.shape
        xt = x.reshape(-1, D)
        T = xt.shape[0]
        scores = jax.nn.sigmoid(xt.astype(jnp.float32) @ gate_w.T)
        biased = scores + gate_b
        _, idx = lax.top_k(biased, TOPK)
        w = jnp.take_along_axis(scores, idx, axis=-1)
        w = w / jnp.sum(w, axis=-1, keepdims=True)
        w = w * ROUTE_SCALE
        comb = jnp.zeros((T, N_EXPERTS), jnp.float32)
        comb = comb.at[jnp.arange(T)[:, None], idx].add(w)
        comb = comb.astype(x.dtype)

        def expert_body(y, args):
            w13_e, w2_e, c_e = args
            h = _silu_and_mul(xt @ w13_e.T)
            return (y + c_e[:, None] * (h @ w2_e.T), None)
        y, _ = lax.scan(expert_body, jnp.zeros_like(xt), (w13, w2, comb.T))
        y = y + _silu_and_mul(xt @ w13_s.T) @ w2_s.T
        return y.astype(x.dtype).reshape(B, S, D)
    x = x + _L0_xattn_ref(_layernorm(x, axis=-1), ctx_1024, ctx_1024, fside_Bx1xSxS2_0, L0_xattn_Wq, L0_xattn_Wk, L0_xattn_Wv, L0_xattn_Wo, 16)
    x = x + _L0_ffn_ref(_layernorm(x, axis=-1), L0_ffn_input_ids, L0_ffn_gate_w, L0_ffn_gate_b, L0_ffn_w13, L0_ffn_w2, L0_ffn_w13_s, L0_ffn_w2_s)
    return x

_drawn_inputs = setup_inputs


def setup_inputs(seed=0):
    import zlib

    import numpy as np

    out = dict(_drawn_inputs(seed))
    spreads = {}
    factors = {'L0_ffn_gate_w': 8.0,
     'L0_ffn_gate_b': 8.0,
     'L0_ffn_w13': 8.0,
     'L0_ffn_w2': 8.0,
     'L0_ffn_w13_s': 8.0,
     'L0_ffn_w2_s': 8.0}
    for name, (base, spread) in spreads.items():
        noise = np.random.default_rng([zlib.crc32(name.encode()), seed]).standard_normal(out[name].shape)
        drawn = base * np.exp(spread * noise) if base else spread * noise
        out[name] = jnp.asarray(drawn.astype(out[name].dtype))
    for name, factor in factors.items():
        out[name] = (out[name] * factor).astype(out[name].dtype)
    return out
```

```python
from contextlib import ExitStack

import concourse.bass as bass
from concourse import mybir

F32 = mybir.dt.float32
F32R = mybir.dt.float32r
U32 = mybir.dt.uint32
ALU = mybir.AluOpType
ACT = mybir.ActivationFunctionType
AXX = mybir.AxisListType.X

P = 128
EPS = 1e-5
TOPK = 4
ROUTE_SCALE = 2.5
BIG = 3.0e38
DMA = 16


class Ring:

    def __init__(self, make_tensor, make_sem, name, size, shape, dt):
        self.tiles = [make_tensor(f"{name}{i}", shape, dt) for i in range(size)]
        self.sems = [make_sem(f"s_{name}{i}") for i in range(size)]
        self.size = size

    def tile(self, n):
        return self.tiles[n % self.size]

    def sem(self, n):
        return self.sems[n % self.size]

    def wait(self, eng, n):
        eng.wait_ge(self.sem(n), DMA * (n // self.size + 1))


def f32(ap):
    return ap.bitcast(F32)


def split_products(eng, out, left, right, first=True, last=True):
    eng.matmul(out, left[0], right[0], start=first, stop=False)
    eng.matmul(out, left[0], right[1], start=False, stop=False)
    return eng.matmul(out, left[1], right[0], start=False, stop=last)


def attention_phase(nc, ident_dram, x, ctxT, mask, wqT, wkT, wvT, woT, x2):
    B, S, D = x.shape
    INNER = wqT.shape[1]
    DH = 64
    H = INNER // DH
    NT = S // P
    NK = D // P
    NP = H // 2
    NE = INNER // P
    G = B * H

    T_LAG, PV_LAG = 2, 3
    E_RING, PT_RING, QK_RING = 4, 2, 2
    WO_STEP, LN_STEP, XT_STEP, VP_STEP = 4, 5, 8, 9

    with ExitStack() as ctx:
        def sb(name, shape, dt=F32):
            return ctx.enter_context(nc.sbuf_tensor(name, shape, dt))

        def sem(name):
            return ctx.enter_context(nc.semaphore(name))

        def pair_of(name, shape):
            return sb(name + "_hi", shape, F32R), sb(name + "_lo", shape, F32R)

        wq, wv = (pair_of(n, [P, NK, INNER]) for n in ("wq", "wv"))
        wk = pair_of("wk", [P, NK, H, 2, DH])
        wo = pair_of("wo", [P, NE, D])
        stage = sb("stage", [P, INNER])
        chunks = [(w[k * P:(k + 1) * P, :], [part[:, k] for part in parts])
                  for w, parts in ((wkT, wk), (wvT, wv), (wqT, wq)) for k in range(NK)]
        EC = INNER // D
        chunks += [(woT[c * P:(c + EC) * P, :].rearrange("(k p) n -> p k n", p=P), [part[:, c:c + EC, :] for part in wo])
                   for c in range(0, NE, EC)]
        W_K, W_V, W_Q, W_O = NK, 2 * NK, 3 * NK, len(chunks)

        def staged(dst):
            if len(dst.shape) == 4:
                return [(dst[:, :, r, :], stage[:, :].rearrange("p (h d) -> p h d", h=H)) for r in range(2)]
            if len(dst.shape) == 3:
                return [(dst, stage[:, :].rearrange("p (k n) -> p k n", k=EC))]
            return [(dst, stage[:, :])]

        ident = sb("ident", [P, P])
        x_in = Ring(sb, sem, "x_in", 2, [P, NT, D], F32)
        c_in = Ring(sb, sem, "c_in", 2, [P, NK, S], F32)
        m_in = Ring(sb, sem, "m_in", 2, [P, NT, S], F32)
        s_x2out = [sem(f"s_x2out{i}") for i in range(x_in.size)]
        xn = sb("xn", [P, NT, D])
        xnT = [pair_of(f"xnT{i}", [P, NK, S]) for i in range(2)]
        cT = [pair_of(f"cT{i}", [P, NK, S]) for i in range(2)]
        V = [pair_of(f"V{i}", [P, NT, NP, 3, DH]) for i in range(2)]
        att = pair_of("att", [P, NE, S])
        q_st = [sb(f"q_st{i}", [P, 2, S], F32R) for i in range(QK_RING)]
        k_hi = [sb(f"k_hi{i}", [P, 2, S], F32R) for i in range(QK_RING)]
        k_lo = [sb(f"k_lo{i}", [P, 2, S], F32R) for i in range(QK_RING)]
        E = [sb(f"E{i}", [P, NT, S]) for i in range(E_RING)]
        PT = [pair_of(f"PT{i}", [P, NT, S]) for i in range(PT_RING)]
        negmax = sb("negmax", [P, E_RING, NT])
        rowsum = sb("rowsum", [P, E_RING, NT])
        rinv = sb("rinv", [P, E_RING, NT])
        st6 = sb("st6", [P, NT, 6])
        mv = sb("mv", [P, NT, 2])
        veps = sb("veps", [P, NT])
        rstd = sb("rstd", [P, NT])
        mhalf = sb("mhalf", [P, NT])

        pj = [ctx.enter_context(nc.psum_tensor(f"pj{i}", [P, 512], F32)) for i in range(2)]
        pS = [ctx.enter_context(nc.psum_tensor(f"pS{i}", [P, NT, S], F32)) for i in range(2)]
        pT = [ctx.enter_context(nc.psum_tensor(f"pT{i}", [P, NT, S], F32)) for i in range(2)]
        pV = [ctx.enter_context(nc.psum_tensor(f"pV{i}", [P, 512], F32)) for i in range(2)]

        s_ident, s_stage, s_whi, s_wlo = sem("s_ident"), sem("s_stage"), sem("s_whi"), sem("s_wlo")
        s_const = sem("s_const")
        s_pj, s_hi, s_pjfree = sem("s_pj"), sem("s_hi"), sem("s_pjfree")
        s_S, s_T, s_PV = sem("s_S"), sem("s_T"), sem("s_PV")
        s_max, s_exp, s_rinv, s_norm = sem("s_max"), sem("s_exp"), sem("s_rinv"), sem("s_norm")
        s_pthi, s_ptlo, s_atthi, s_attlo = sem("s_pthi"), sem("s_ptlo"), sem("s_atthi"), sem("s_attlo")
        s_bn, s_agg, s_veps, s_rstd, s_xn = sem("s_bn"), sem("s_agg"), sem("s_veps"), sem("s_rstd"), sem("s_xn")
        s_chi, s_clo = sem("s_chi"), sem("s_clo")

        uses, number = {}, {}

        def use(step, what):
            number[what] = len(number)
            uses.setdefault(step, []).append(what)

        PRE = -1
        use(PRE, ("xT", 0))
        for part in range(2 * NT):
            use(PRE, ("v", 0, part))
        use(PRE, ("q", 0))
        use(PRE, ("k", 0))
        for g in range(G + PV_LAG + WO_STEP + 1):
            b, h = divmod(g, H)
            if g < G and h % 2 == 0 and g // 2 + 1 < G // 2:
                use(g, ("q", g // 2 + 1))
                use(g, ("k", g // 2 + 1))
            if h == WO_STEP and b >= 1:
                use(g, ("wo", b - 1))
            if h == XT_STEP and b + 1 < B:
                use(g, ("xT", b + 1))
            if VP_STEP <= h < VP_STEP + 2 * NT and b + 1 < B:
                use(g, ("v", b + 1, h - VP_STEP))
        steps = range(PRE, max(uses) + 1)

        def qk_buf(pair):
            return pair % QK_RING

        block = ctx.enter_context(nc.Block())

        @block.sync
        def _(sp):
            sp.dma_start(ident[:, :], ident_dram).then_inc(s_ident, DMA)

            def load(n):
                if n >= B:
                    return
                if n >= x_in.size:
                    sp.wait_ge(s_x2out[n % x_in.size], DMA * (n // x_in.size))
                sp.dma_start(x_in.tile(n)[:, :, :], x[n].rearrange("(t p) d -> p t d", p=P)).then_inc(x_in.sem(n), DMA)
                if n >= 2:
                    sp.wait_ge(s_clo, n - 1)
                sp.dma_start(c_in.tile(n)[:, :, :], ctxT[n].rearrange("(k p) s -> p k s", p=P)).then_inc(c_in.sem(n), DMA)
                if n >= 2:
                    sp.wait_ge(s_max, H * (n - 1))
                sp.dma_start(m_in.tile(n)[:, :, :], mask[n, 0].rearrange("(t p) s -> p t s", p=P)).then_inc(m_in.sem(n), DMA)

            load(0)
            for i, (w, parts) in enumerate(chunks):
                if i:
                    sp.wait_ge(s_wlo, i)
                dst = stage[:, :] if len(w.shape) == 2 else stage[:, :].rearrange("p (k n) -> p k n", k=EC)
                sp.dma_start(dst, w).then_inc(s_stage, DMA)
            load(1)
            for b in range(B):
                sp.wait_ge(s_pjfree, number[("wo", b)] + 1)
                sp.dma_start(x2[b].rearrange("(t p) d -> p t d", p=P), x_in.tile(b)[:, :, :]).then_inc(
                    s_x2out[b % x_in.size], DMA)
                load(b + 2)
            for b in range(max(0, B - x_in.size), B):
                sp.wait_ge(s_x2out[b % x_in.size], DMA * (b // x_in.size + 1))

        @block.gpsimd
        def _(pool):
            pool.memset(mhalf[:, :], -0.5).then_inc(s_const, 1)
            for pair in V:
                for part in pair:
                    pool.memset(f32(part[:, :, :, 1, :]), 0.0).then_inc(s_const, 1)
            pool.wait_ge(s_const, 5)

            def split_context(b):
                if b >= 2:
                    pool.wait_ge(s_pj, number[("k", b * NP - NP - 1)] + 1)
                c_in.wait(pool, b)
                hi, lo = cT[b % 2]
                pool.tensor_copy(hi[:, :, :], c_in.tile(b)[:, :, :]).then_inc(s_chi, 1)
                pool.wait_ge(s_chi, b + 1)
                pool.tensor_tensor(lo[:, :, :], c_in.tile(b)[:, :, :], f32(hi[:, :, :]), ALU.subtract).then_inc(s_clo, 1)

            def inverse_std(b):
                pool.wait_ge(s_veps, b + 1)
                pool.tensor_tensor(rstd[:, :], veps[:, :], mhalf[:, :], ALU.pow).then_inc(s_rstd, 1)

            inverse_std(0)
            split_context(0)
            for g in range(G):
                b, h = divmod(g, H)
                pool.wait_ge(s_exp, g + 1)
                pool.wait_ge(s_rinv, g + 1)
                e, r = E[g % E_RING], g % E_RING
                for t in range(NT):
                    last = pool.tensor_scalar(e[:, t, :], e[:, t, :], rinv[:, r, t:t + 1], 1.0, ALU.mult, ALU.mult)
                last.then_inc(s_norm, 1)
                if h == LN_STEP and b + 1 < B:
                    split_context(b + 1)
                    inverse_std(b + 1)

        @block.tensor
        def _(pe):
            def bank(what):
                n = number[what]
                if n >= 2:
                    pe.wait_ge(s_pjfree, n - 1)
                return pj[n % 2]

            def fill(what):
                kind, n = what[0], what[1]
                ps = bank(what)
                if kind == "xT":
                    pe.wait_ge(s_xn, n + 1)
                    for t in range(NT):
                        for k in range(NK):
                            last = pe.transpose(ps[:, k * S + t * P:k * S + (t + 1) * P],
                                                xn[:, t, k * P:(k + 1) * P], ident[:, :])
                elif kind == "v":
                    pe.wait_ge(s_clo, n + 1)
                    if n == 0:
                        pe.wait_ge(s_wlo, W_V)
                    t, half = divmod(what[2], 2)
                    for k in range(NK):
                        last = split_products(
                            pe, ps[:, :], [c[:, k, t * P:(t + 1) * P] for c in cT[n % 2]],
                            [w[:, k, half * 512:(half + 1) * 512] for w in wv], k == 0, k == NK - 1)
                elif kind == "q":
                    b, j = divmod(n, NP)
                    if n == 0:
                        pe.wait_ge(s_wlo, W_Q)
                    pe.wait_ge(s_pjfree, number[("xT", b)] + 1)
                    for k in range(NK):
                        last = split_products(
                            pe, ps[:, 0:S], [w[:, k, j * P:(j + 1) * P] for w in wq],
                            [a[:, k, :] for a in xnT[b % 2]], k == 0, k == NK - 1)
                elif kind == "k":
                    b, j = divmod(n, NP)
                    pe.wait_ge(s_clo, b + 1)
                    for a in range(2):
                        for k in range(NK):
                            last = split_products(pe, ps[:, a * S:(a + 1) * S], [w[:, k, 2 * j + a, :, :] for w in wk],
                                                  [c[:, k, :] for c in cT[b % 2]], k == 0, k == NK - 1)
                else:
                    if n == 0:
                        pe.wait_ge(s_wlo, W_O)
                    pe.wait_ge(s_attlo, (n + 1) * NP)
                    for t in range(NT):
                        for k in range(NE):
                            last = split_products(
                                pe, ps[:, t * D:(t + 1) * D], [a[:, k, t * P:(t + 1) * P] for a in att],
                                [w[:, k, :] for w in wo], k == 0, k == NE - 1)
                last.then_inc(s_pj, 1)

            def scores(g):
                pair, a = divmod(g, 2)
                if a == 0:
                    pe.wait_ge(s_pjfree, number[("k", pair)] + 1)
                if g >= 2:
                    pe.wait_ge(s_max, g - 1)
                q = q_st[qk_buf(pair)]
                for t in range(NT):
                    left = q[:, a, t * P:(t + 1) * P]
                    pe.matmul(pS[g % 2][:, t, :], left, k_hi[qk_buf(pair)][:, a, :], start=True, stop=False)
                    last = pe.matmul(pS[g % 2][:, t, :], left, k_lo[qk_buf(pair)][:, a, :], start=False, stop=True)
                last.then_inc(s_S, 1)

            def transpose_probs(g):
                pe.wait_ge(s_norm, g + 1)
                if g >= 2:
                    pe.wait_ge(s_ptlo, g - 1)
                e = E[g % E_RING]
                for t in range(NT):
                    for k in range(NT):
                        last = pe.transpose(pT[g % 2][:, k, t * P:(t + 1) * P], e[:, t, k * P:(k + 1) * P], ident[:, :])
                last.then_inc(s_T, 1)

            def values(g):
                pair, a = divmod(g, 2)
                b, j = divmod(pair, NP)
                pe.wait_ge(s_ptlo, g + 1)
                if j == 0 and a == 0:
                    pe.wait_ge(s_pjfree, number[("v", b, 2 * NT - 1)] + 1)
                if a == 0 and pair >= 2:
                    pe.wait_ge(s_attlo, pair - 1)
                for k in range(NT):
                    last = split_products(
                        pe, pV[pair % 2][:, 0:S], [v[:, k, j, a:a + 2, :] for v in V[b % 2]],
                        [p[:, k, :] for p in PT[g % PT_RING]], a == 0 and k == 0, a == 1 and k == NT - 1)
                last.then_inc(s_PV, 1)

            pe.wait_ge(s_ident, DMA)
            pe.wait_ge(s_wlo, W_K)
            pe.wait_ge(s_const, 5)
            for g in steps:
                if 0 <= g < G:
                    scores(g)
                if 0 <= g - T_LAG < G:
                    transpose_probs(g - T_LAG)
                for what in uses.get(g, ()):
                    fill(what)
                if 0 <= g - PV_LAG < G:
                    values(g - PV_LAG)

        @block.scalar
        def _(act):
            for i, (w, parts) in enumerate(chunks):
                act.wait_ge(s_stage, DMA * (i + 1))
                for dst, src in staged(parts[0]):
                    last = act.activation(dst, src, ACT.Copy)
                last.then_inc(s_whi, 1)

            def hi_part(what):
                kind, n = what[0], what[1]
                if kind == "wo":
                    return
                act.wait_ge(s_pj, number[what] + 1)
                ps = pj[number[what] % 2]
                if kind == "xT":
                    if n >= 2:
                        act.wait_ge(s_pj, number[("q", (n - 1) * NP - 1)] + 1)
                    last = act.activation(xnT[n % 2][0][:, :, :], ps[:, :].rearrange("p (k s) -> p k s", k=NK), ACT.Copy)
                elif kind == "v":
                    if n >= 2 and what[2] == 0:
                        act.wait_ge(s_PV, (n - 1) * H)
                    t, half = divmod(what[2], 2)
                    j = half * NP // 2
                    last = act.activation(V[n % 2][0][:, t, j:j + NP // 2, 0:3:2, :],
                                          ps[:, :].rearrange("p (j a d) -> p j a d", a=2, d=DH), ACT.Copy)
                elif kind == "q":
                    if n >= QK_RING:
                        act.wait_ge(s_S, 2 * (n - QK_RING + 1))
                    q = q_st[qk_buf(n)]
                    act.activation(q[0:DH, 0, :], ps[0:DH, 0:S], ACT.Copy)
                    last = act.activation(q[DH:P, 1, :], ps[DH:P, 0:S], ACT.Copy)
                else:
                    if n >= QK_RING:
                        act.wait_ge(s_S, 2 * (n - QK_RING + 1))
                    last = act.activation(k_hi[qk_buf(n)][:, :, :], ps[:, :].rearrange("p (a s) -> p a s", a=2), ACT.Copy)
                last.then_inc(s_hi, 1)

            for g in steps:
                if 0 <= g < G:
                    act.wait_ge(s_max, g + 1)
                    if g >= E_RING:
                        act.wait_ge(s_rinv, g - E_RING + 1)
                    r = g % E_RING
                    for t in range(NT):
                        last = act.activation(E[r][:, t, :], E[r][:, t, :], ACT.Exp, bias=negmax[:, r, t:t + 1],
                                              scale=-1.0, accum_out=rowsum[:, r, t:t + 1])
                    last.then_inc(s_exp, 1)
                if 0 <= g - T_LAG < G:
                    n = g - T_LAG
                    act.wait_ge(s_T, n + 1)
                    if n >= PT_RING:
                        act.wait_ge(s_PV, n - PT_RING + 1)
                    act.activation(PT[n % PT_RING][0][:, :, :], pT[n % 2][:, :, :], ACT.Copy).then_inc(s_pthi, 1)
                for what in uses.get(g, ()):
                    hi_part(what)
                n = g - PV_LAG
                if 0 <= n < G and n % 2:
                    pair = n // 2
                    b, j = divmod(pair, NP)
                    act.wait_ge(s_PV, n + 1)
                    if b and j == 0:
                        act.wait_ge(s_pj, number[("wo", b - 1)] + 1)
                    act.activation(att[0][:, j, :], pV[pair % 2][:, 0:S], ACT.Copy).then_inc(s_atthi, 1)

        @block.vector
        def _(dve):
            his = [0]

            def normalise(b):
                x_in.wait(dve, b)
                xb = x_in.tile(b)
                for t in range(NT):
                    last = dve.bn_stats(st6[:, t, :], xb[:, t, :])
                last.then_inc(s_bn, 1)
                dve.wait_ge(s_bn, b + 1)
                for t in range(NT):
                    last = dve.bn_aggr(mv[:, t, :], st6[:, t, :])
                last.then_inc(s_agg, 1)
                dve.wait_ge(s_agg, b + 1)
                dve.tensor_scalar(veps[:, :], mv[:, :, 1], EPS, None, ALU.add).then_inc(s_veps, 1)

            def apply_norm(b):
                dve.wait_ge(s_rstd, b + 1)
                if b:
                    dve.wait_ge(s_pj, number[("xT", b - 1)] + 1)
                for t in range(NT):
                    last = dve.tensor_scalar(xn[:, t, :], x_in.tile(b)[:, t, :], mv[:, t, 0:1], rstd[:, t:t + 1],
                                             ALU.subtract, ALU.mult)
                last.then_inc(s_xn, 1)

            def lo_part(what):
                kind, n = what[0], what[1]
                ps = pj[number[what] % 2]
                if kind == "wo":
                    dve.wait_ge(s_pj, number[what] + 1)
                    xb = x_in.tile(n)
                    last = dve.tensor_tensor(xb[:, :, :], ps[:, :].rearrange("p (t d) -> p t d", t=NT), xb[:, :, :], ALU.add)
                    last.then_inc(s_pjfree, 1)
                    return
                his[0] += 1
                dve.wait_ge(s_hi, his[0])
                if kind == "xT":
                    hi, lo = xnT[n % 2]
                    last = dve.tensor_tensor(lo[:, :, :], ps[:, :].rearrange("p (k s) -> p k s", k=NK), f32(hi[:, :, :]), ALU.subtract)
                elif kind == "v":
                    t, half = divmod(what[2], 2)
                    j = half * NP // 2
                    hi, lo = (v[:, t, j:j + NP // 2, 0:3:2, :] for v in V[n % 2])
                    last = dve.tensor_tensor(lo, ps[:, :].rearrange("p (j a d) -> p j a d", a=2, d=DH), f32(hi), ALU.subtract)
                elif kind == "q":
                    q = q_st[qk_buf(n)]
                    dve.tensor_tensor(q[DH:P, 0, :], ps[0:DH, 0:S], f32(q[0:DH, 0, :]), ALU.subtract)
                    last = dve.tensor_tensor(q[0:DH, 1, :], ps[DH:P, 0:S], f32(q[DH:P, 1, :]), ALU.subtract)
                else:
                    last = dve.tensor_tensor(k_lo[qk_buf(n)][:, :, :], ps[:, :].rearrange("p (a s) -> p a s", a=2),
                                             f32(k_hi[qk_buf(n)][:, :, :]), ALU.subtract)
                last.then_inc(s_pjfree, 1)

            def inverse_sums(g):
                r = g % E_RING
                dve.wait_ge(s_exp, g + 1)
                if g >= E_RING:
                    dve.wait_ge(s_norm, g - E_RING + 1)
                dve.reciprocal(rinv[:, r, :], rowsum[:, r, :]).then_inc(s_rinv, 1)

            normalise(0)
            apply_norm(0)
            for i, (w, parts) in enumerate(chunks):
                dve.wait_ge(s_whi, i + 1)
                for (hi, src), (lo, _) in zip(staged(parts[0]), staged(parts[1])):
                    last = dve.tensor_tensor(lo, src, f32(hi), ALU.subtract)
                last.then_inc(s_wlo, 1)
            for g in steps:
                b, h = divmod(g, H)
                if 0 <= g < G:
                    r = g % E_RING
                    dve.wait_ge(s_S, g + 1)
                    if h == 0:
                        m_in.wait(dve, b)
                    if g >= E_RING:
                        dve.wait_ge(s_T, g - E_RING + 1)
                    for t in range(NT):
                        last = dve.tensor_tensor_reduce(
                            out=E[r][:, t, :], in0=pS[g % 2][:, t, :], in1=m_in.tile(b)[:, t, :], scale=-1.0,
                            scalar=BIG, op0=ALU.add, op1=ALU.min, accum_out=negmax[:, r, t:t + 1])
                    last.then_inc(s_max, 1)
                if 0 <= g - 1 < G:
                    inverse_sums(g - 1)
                if 0 <= g - T_LAG < G:
                    n = g - T_LAG
                    dve.wait_ge(s_pthi, n + 1)
                    hi, lo = PT[n % PT_RING]
                    dve.tensor_tensor(lo[:, :, :], pT[n % 2][:, :, :], f32(hi[:, :, :]), ALU.subtract).then_inc(s_ptlo, 1)
                for what in uses.get(g, ()):
                    lo_part(what)
                n = g - PV_LAG
                if 0 <= n < G and n % 2:
                    pair = n // 2
                    j = pair % NP
                    dve.wait_ge(s_atthi, pair + 1)
                    dve.tensor_tensor(att[1][:, j, :], pV[pair % 2][:, 0:S], f32(att[0][:, j, :]), ALU.subtract).then_inc(s_attlo, 1)
                if 0 <= g < G and b + 1 < B:
                    if h == LN_STEP:
                        normalise(b + 1)
                    if h == XT_STEP - 1:
                        apply_norm(b + 1)


def expert_phase(nc, ident_dram, sel_dram, iota_dram, x2, gate_wT, gate_b, w13T, w2T, w13_sT, w2_sT, out):
    B, S, D = x2.shape
    N_EXP = gate_wT.shape[1]
    INTER = w2T.shape[1]
    NX = N_EXP + 1
    NT, NK = S // P, D // P
    ND = N_EXP * 2

    with ExitStack() as ctx:
        def sb(name, shape, dt=F32):
            return ctx.enter_context(nc.sbuf_tensor(name, shape, dt))

        def sem(name):
            return ctx.enter_context(nc.semaphore(name))

        def pair_of(name, shape):
            return sb(name + "_hi", shape, F32R), sb(name + "_lo", shape, F32R)

        w13 = pair_of("w13", [P, NX, NK, 2 * INTER])
        w2 = pair_of("w2", [P, NX, D])
        gw = pair_of("gw", [P, NK, N_EXP])
        stage = Ring(sb, sem, "wstage", 4, [P, NK * 2 * INTER + D], F32)
        gw_raw = sb("gw_raw", [P, NK, N_EXP])
        gb = sb("gb", [P, NT, N_EXP])
        ident = sb("ident2", [P, P])
        sel_raw = sb("sel_raw", [P, N_EXP, P])
        sel = sb("sel", [P, N_EXP, P], F32R)
        iota = sb("iota", [P, NT, TOPK, N_EXP])
        x_in = Ring(sb, sem, "y_in", 3, [P, NT, D], F32)
        s_out = [sem(f"s_out{i}") for i in range(3)]
        xn = sb("xn2", [P, NT, D])
        xnT = [pair_of(f"xnT2_{i}", [P, NK, S]) for i in range(2)]
        st6, mv = sb("st6b", [P, NT, 6]), sb("mvb", [P, NT, 2])
        veps, rstd, mhalf = sb("vepsb", [P, NT]), sb("rstdb", [P, NT]), sb("mhalfb", [P, NT])
        lgT = sb("lgT", [N_EXP, S])
        sc, bi = sb("sc", [P, NT, N_EXP]), sb("bi", [P, NT, N_EXP])
        top, topi = sb("top", [P, NT, 8]), sb("topi", [P, NT, 8], U32)
        topf = sb("topf", [P, NT, TOPK])
        onehot = sb("onehot", [P, NT, TOPK, N_EXP])
        chosen, wsum, wrec = sb("chosen", [P, NT, N_EXP]), sb("wsum", [P, NT]), sb("wrec", [P, NT])
        wch, comb = sb("wch", [P, NT, N_EXP]), sb("comb", [P, NT, N_EXP])
        csplit = sb("csplit", [P, NT, ND])
        chi = sb("chi", [P, NT, N_EXP], F32R)
        combT = [sb(f"combT{i}", [P, S], F32R) for i in range(2)]
        sig = [sb(f"sig{i}", [P, S]) for i in range(2)]
        hid = [sb(f"hid{i}", [P, S]) for i in range(2)]
        hsp = [pair_of(f"hsp{i}", [P, S]) for i in range(3)]

        pGU = [ctx.enter_context(nc.psum_tensor(f"pGU{i}", [P, 2, S], F32)) for i in range(2)]
        pC = [ctx.enter_context(nc.psum_tensor(f"pC{i}", [P, 512], F32)) for i in range(2)]
        pY = [ctx.enter_context(nc.psum_tensor(f"pY{i}", [P, 512], F32)) for i in range(NT)]
        pM = [ctx.enter_context(nc.psum_tensor(f"pM{i}", [P, 512], F32)) for i in range(2)]

        s_ld, s_const, s_cst2 = sem("t_ld"), sem("t_const"), sem("t_const2")
        s_whi, s_wlo = sem("t_whi"), sem("t_wlo")
        s_veps, s_rstd, s_xn = sem("t_veps"), sem("t_rstd"), sem("t_xn")
        s_xT, s_xhi, s_xlo = sem("t_xT"), sem("t_xhi"), sem("t_xlo")
        s_lg, s_lgc, s_lgt, s_sc = sem("t_lg"), sem("t_lgc"), sem("t_lgt"), sem("t_sc")
        s_comb, s_cT, s_combT = sem("t_comb"), sem("t_cT"), sem("t_combT")
        s_GU, s_C, s_sig, s_hid, s_hhi, s_hlo, s_y, s_yout = (
            sem(n) for n in ("t_GU", "t_C", "t_sig", "t_hid", "t_hhi", "t_hlo", "t_y", "t_yout"))
        s_chain = sem("t_chain")

        XI = [(b, e) for b in range(B) for e in range(NX)]
        N = len(XI)
        W2_LAG = 2
        LN_AT, XT_AT, LG_AT, LGT_AT, RT_AT, CT_AT = 1, 4, 6, 8, 10, 13

        block = ctx.enter_context(nc.Block())

        @block.sync
        def _(sp):
            sp.dma_start(ident[:, :], ident_dram).then_inc(s_ld, DMA)
            sp.dma_start(sel_raw[:, :, :], sel_dram).then_inc(s_ld, DMA)
            sp.dma_start(iota[:, :, :, :], iota_dram).then_inc(s_ld, DMA)
            sp.dma_start(gw_raw[:, :, :], gate_wT.rearrange("(k p) e -> p k e", p=P)).then_inc(s_ld, DMA)
            for t in range(NT):
                sp.dma_start(gb[:, t, :], gate_b.partition_broadcast(P)).then_inc(s_ld, DMA)

            def load(n):
                if n < B:
                    if n >= 3:
                        sp.wait_ge(s_out[n % 3], DMA * (n // 3))
                    sp.dma_start(x_in.tile(n)[:, :, :], x2[n].rearrange("(t p) d -> p t d", p=P)).then_inc(x_in.sem(n), DMA)

            load(0)
            load(1)
            W13 = NK * 2 * INTER
            for e in range(NX):
                if e >= stage.size:
                    sp.wait_ge(s_wlo, e - stage.size + 1)
                a = w13T[e] if e < N_EXP else w13_sT
                c = w2T[e] if e < N_EXP else w2_sT
                sp.dma_start(stage.tile(e)[:, 0:W13].rearrange("p (k n) -> p k n", k=NK),
                             a.rearrange("(k p) n -> p k n", p=P)).then_inc(stage.sem(e), DMA)
                sp.dma_start(stage.tile(e)[:, W13:W13 + D], c).then_inc(stage.sem(e), DMA)
            load(2)
            for b in range(B):
                sp.wait_ge(s_yout, b + 1)
                sp.dma_start(out[b].rearrange("(t p) d -> p t d", p=P), x_in.tile(b)[:, :, :]).then_inc(s_out[b % 3], DMA)
                load(b + 3)
            for b in range(max(0, B - 3), B):
                sp.wait_ge(s_out[b % 3], DMA * (b // 3 + 1))

        def weights_here(eng, e):
            eng.wait_ge(stage.sem(e), 2 * DMA * (e // stage.size + 1))

        def staged(e):
            W13 = NK * 2 * INTER
            t = stage.tile(e)
            return t[:, 0:W13].rearrange("p (k n) -> p k n", k=NK), t[:, W13:W13 + D]

        @block.gpsimd
        def _(pool):
            pool.memset(mhalf[:, :], -0.5).then_inc(s_const, 1)
            for c in combT:
                pool.memset(f32(c[:, :]), 0.0).then_inc(s_const, 1)
            pool.wait_ge(s_const, 3)

            def inverse_std(b):
                pool.wait_ge(s_veps, b + 1)
                pool.tensor_tensor(rstd[:, :], veps[:, :], mhalf[:, :], ALU.pow).then_inc(s_rstd, 1)

            inverse_std(0)
            for i, (b, e) in enumerate(XI):
                pool.wait_ge(s_hhi, i + 1)
                hi, lo = hsp[i % 3]
                if i >= 3:
                    pool.wait_ge(s_y, i - 2)
                pool.tensor_tensor(lo[:, :], hid[i % 2][:, :], f32(hi[:, :]), ALU.subtract).then_inc(s_hlo, 1)
                if e == LN_AT and b + 1 < B:
                    inverse_std(b + 1)

        @block.tensor
        def _(pe):
            def transposed_x(b):
                pe.wait_ge(s_xn, b + 1)
                for t in range(NT):
                    for k in range(NK):
                        last = pe.transpose(pM[0][:, k * S + t * P:k * S + (t + 1) * P],
                                            xn[:, t, k * P:(k + 1) * P], ident[:, :])
                last.then_inc(s_xT, 1)

            def logits(b):
                pe.wait_ge(s_xlo, b + 1)
                if b:
                    pe.wait_ge(s_combT, b)
                for k in range(NK):
                    last = split_products(pe, pM[1][0:N_EXP, 0:S], [g[:, k, :] for g in gw],
                                          [a[:, k, :] for a in xnT[b % 2]], k == 0, k == NK - 1)
                last.then_inc(s_lg, 1)

            def logits_by_token(b):
                pe.wait_ge(s_lgc, b + 1)
                for t in range(NT):
                    last = pe.transpose(pM[1][:, t * N_EXP:(t + 1) * N_EXP], lgT[:, t * P:(t + 1) * P],
                                        ident[0:N_EXP, 0:N_EXP])
                last.then_inc(s_lgt, 1)

            def comb_by_expert(b):
                pe.wait_ge(s_comb, b + 1)
                for t in range(NT):
                    last = pe.transpose(pM[1][0:ND, t * P:(t + 1) * P], csplit[:, t, :], ident[:, :])
                last.then_inc(s_cT, 1)

            prepare = {XT_AT: transposed_x, LG_AT: logits, LGT_AT: logits_by_token, CT_AT: comb_by_expert}
            pe.wait_ge(s_ld, 6 * DMA)
            pe.wait_ge(s_cst2, 3)
            for at in sorted(prepare):
                prepare[at](0)
            for i in range(N + W2_LAG):
                if i < N:
                    b, e = XI[i]
                    if b == 0:
                        pe.wait_ge(s_wlo, e + 1)
                    if i >= 2:
                        pe.wait_ge(s_hid, i - 1)
                    for m in range(2):
                        for k in range(NK):
                            last = split_products(pe, pGU[i % 2][:, m, :],
                                                  [w[:, e, k, m * INTER:(m + 1) * INTER] for w in w13],
                                                  [a[:, k, :] for a in xnT[b % 2]], k == 0, k == NK - 1)
                    last.then_inc(s_GU, 1)
                    if e < N_EXP:
                        if e == 0:
                            pe.wait_ge(s_combT, b + 1)
                        pe.matmul(pC[i % 2][:, 0:S], sel[:, e, :], combT[b % 2][:, :], start=True, stop=True).then_inc(s_C, 1)
                    if e in prepare and b + 1 < B:
                        prepare[e](b + 1)
                if i >= W2_LAG:
                    n = i - W2_LAG
                    b, e = XI[n]
                    pe.wait_ge(s_hlo, n + 1)
                    if e == 0 and b:
                        pe.wait_ge(s_yout, b)
                    for t in range(NT):
                        last = split_products(pe, pY[t][:, 0:D], [h[:, t * P:(t + 1) * P] for h in hsp[n % 3]],
                                              [w[:, e, :] for w in w2], e == 0, e == NX - 1)
                    last.then_inc(s_y, 1)

        @block.scalar
        def _(act):
            act.wait_ge(s_ld, 6 * DMA)
            act.activation(gw[0][:, :, :], gw_raw[:, :, :], ACT.Copy).then_inc(s_cst2, 1)
            act.activation(sel[:, :, :], sel_raw[:, :, :], ACT.Copy).then_inc(s_cst2, 1)

            def x_hi(b):
                act.wait_ge(s_xT, b + 1)
                if b >= 2:
                    act.wait_ge(s_GU, (b - 1) * NX)
                act.activation(xnT[b % 2][0][:, :, :], pM[0][:, :].rearrange("p (k s) -> p k s", k=NK), ACT.Copy).then_inc(s_xhi, 1)

            def logit_copy(b):
                act.wait_ge(s_lg, b + 1)
                act.activation(lgT[:, :], pM[1][0:N_EXP, 0:S], ACT.Copy).then_inc(s_lgc, 1)

            def gate_scores(b):
                act.wait_ge(s_lgt, b + 1)
                if b:
                    act.wait_ge(s_comb, b)
                act.activation(sc[:, :, :], pM[1][:, 0:NT * N_EXP].rearrange("p (t e) -> p t e", t=NT),
                               ACT.Sigmoid).then_inc(s_sc, 1)

            def weight_hi(e):
                weights_here(act, e)
                a, c = staged(e)
                act.activation(w13[0][:, e, :, :], a, ACT.Copy)
                act.activation(w2[0][:, e, :], c, ACT.Copy).then_inc(s_whi, 1)

            def hidden_hi(i):
                act.wait_ge(s_hid, i + 1)
                if i >= 3:
                    act.wait_ge(s_y, i - 2)
                act.activation(hsp[i % 3][0][:, :], hid[i % 2][:, :], ACT.Copy).then_inc(s_hhi, 1)

            prepare = {XT_AT: x_hi, LG_AT: logit_copy, LGT_AT: gate_scores}
            for at in sorted(prepare):
                prepare[at](0)
            weight_hi(0)
            weight_hi(1)
            for i, (b, e) in enumerate(XI):
                if b == 0 and e + 2 < NX:
                    weight_hi(e + 2)
                act.wait_ge(s_GU, i + 1)
                if i >= 2:
                    act.wait_ge(s_hid, i - 1)
                act.activation(sig[i % 2][:, :], pGU[i % 2][:, 0, :], ACT.Sigmoid).then_inc(s_sig, 1)
                if e in prepare and b + 1 < B:
                    prepare[e](b + 1)
                if i:
                    hidden_hi(i - 1)
            hidden_hi(N - 1)

        @block.vector
        def _(dve):
            chain = [0]

            def then(ins):
                chain[0] += 1
                ins.then_inc(s_chain, 1)
                dve.wait_ge(s_chain, chain[0])

            def statistics(b):
                x_in.wait(dve, b)
                xb = x_in.tile(b)
                dve.bn_stats(st6[:, 0, :], xb[:, 0, :])
                then(dve.bn_stats(st6[:, 1, :], xb[:, 1, :]))
                dve.bn_aggr(mv[:, 0, :], st6[:, 0, :])
                then(dve.bn_aggr(mv[:, 1, :], st6[:, 1, :]))
                dve.tensor_scalar(veps[:, :], mv[:, :, 1], EPS, None, ALU.add).then_inc(s_veps, 1)

            def apply_norm(b):
                dve.wait_ge(s_rstd, b + 1)
                if b:
                    dve.wait_ge(s_xT, b)
                for t in range(NT):
                    last = dve.tensor_scalar(xn[:, t, :], x_in.tile(b)[:, t, :], mv[:, t, 0:1], rstd[:, t:t + 1],
                                             ALU.subtract, ALU.mult)
                last.then_inc(s_xn, 1)

            def x_lo(b):
                dve.wait_ge(s_xhi, b + 1)
                hi, lo = xnT[b % 2]
                dve.tensor_tensor(lo[:, :, :], pM[0][:, :].rearrange("p (k s) -> p k s", k=NK), f32(hi[:, :, :]),
                                  ALU.subtract).then_inc(s_xlo, 1)

            def route(b):
                dve.wait_ge(s_sc, b + 1)
                then(dve.tensor_tensor(bi[:, :, :], sc[:, :, :], gb[:, :, :], ALU.add))
                dve.max(top[:, 0, :], bi[:, 0, :])
                then(dve.max(top[:, 1, :], bi[:, 1, :]))
                dve.max_index(topi[:, 0, :], top[:, 0, :], bi[:, 0, :])
                then(dve.max_index(topi[:, 1, :], top[:, 1, :], bi[:, 1, :]))
                then(dve.tensor_copy(topf[:, :, :], topi[:, :, 0:TOPK]))
                then(dve.tensor_tensor(onehot[:, :, :, :], iota[:, :, :, :],
                                       topf[:, :, :].unsqueeze(3).broadcast_to([P, NT, TOPK, N_EXP]), ALU.is_equal))
                then(dve.reduce_sum(chosen[:, :, :], onehot[:, :, :, :].rearrange("p t j e -> p t e j"), AXX))
                then(dve.tensor_tensor(wch[:, :, :], chosen[:, :, :], sc[:, :, :], ALU.mult))
                then(dve.reduce_sum(wsum[:, :], wch[:, :, :], AXX))
                then(dve.reciprocal(wrec[:, :], wsum[:, :]))
                for t in range(NT):
                    last = dve.tensor_scalar(comb[:, t, :], wch[:, t, :], wrec[:, t:t + 1], ROUTE_SCALE, ALU.mult, ALU.mult)
                then(last)
                then(dve.tensor_copy(chi[:, :, :], comb[:, :, :]))
                if b:
                    dve.wait_ge(s_cT, b)
                dve.tensor_copy(csplit[:, :, 0:N_EXP], f32(chi[:, :, :]))
                dve.tensor_tensor(csplit[:, :, N_EXP:ND], comb[:, :, :], f32(chi[:, :, :]), ALU.subtract).then_inc(s_comb, 1)

            def comb_rows(b):
                dve.wait_ge(s_cT, b + 1)
                if b >= 2:
                    dve.wait_ge(s_C, (b - 1) * N_EXP)
                dve.tensor_copy(combT[b % 2][0:ND, :], pM[1][0:ND, 0:S]).then_inc(s_combT, 1)

            def weight_lo(e):
                dve.wait_ge(s_whi, e + 1)
                a, c = staged(e)
                dve.tensor_tensor(w13[1][:, e, :, :], a, f32(w13[0][:, e, :, :]), ALU.subtract)
                dve.tensor_tensor(w2[1][:, e, :], c, f32(w2[0][:, e, :]), ALU.subtract).then_inc(s_wlo, 1)

            def finish(b):
                dve.wait_ge(s_y, (b + 1) * NX)
                for t in range(NT):
                    xt = x_in.tile(b)[:, t, :]
                    last = dve.tensor_tensor(xt, pY[t][:, 0:D], xt, ALU.add)
                last.then_inc(s_yout, 1)

            prepare = {LN_AT: statistics, XT_AT - 1: apply_norm, XT_AT: x_lo, RT_AT: route, CT_AT: comb_rows}
            dve.wait_ge(s_const, 3)
            dve.wait_ge(s_cst2, 1)
            dve.tensor_tensor(gw[1][:, :, :], gw_raw[:, :, :], f32(gw[0][:, :, :]), ALU.subtract).then_inc(s_cst2, 1)
            for at in sorted(prepare):
                prepare[at](0)
            weight_lo(0)
            weight_lo(1)
            for i, (b, e) in enumerate(XI):
                if b == 0 and e + 2 < NX:
                    weight_lo(e + 2)
                dve.wait_ge(s_sig, i + 1)
                gu, h = pGU[i % 2], hid[i % 2]
                if i >= 2:
                    dve.wait_ge(s_hlo, i - 1)
                then(dve.tensor_tensor(h[:, :], gu[:, 0, :], sig[i % 2][:, :], ALU.mult))
                if e < N_EXP:
                    then(dve.tensor_tensor(h[:, :], gu[:, 1, :], h[:, :], ALU.mult))
                    dve.wait_ge(s_C, b * N_EXP + e + 1)
                    dve.tensor_tensor(h[:, :], pC[i % 2][:, 0:S], h[:, :], ALU.mult).then_inc(s_hid, 1)
                else:
                    dve.tensor_tensor(h[:, :], gu[:, 1, :], h[:, :], ALU.mult).then_inc(s_hid, 1)
                if e in prepare and b + 1 < B:
                    prepare[e](b + 1)
                if e == W2_LAG - 1 and b:
                    finish(b - 1)
            finish(B - 1)


def program(nc, ins, out):
    x2 = nc.dram_tensor("x_plus_attention", ins["x"].shape, F32, kind="Internal").ap()
    attention_phase(nc, ins["ident"], ins["x"], ins["ctxT"], ins["mask"], ins["wqT"], ins["wkT"], ins["wvT"], ins["woT"], x2)
    expert_phase(nc, ins["ident"], ins["sel"], ins["iota"], x2, ins["gate_wT"], ins["gate_b"], ins["w13T"], ins["w2T"],
                 ins["w13_sT"], ins["w2_sT"], out)


def kernel(**inputs):
    import numpy as np
    import concourse.bacc as bacc
    from concourse.bass_utils import run_bass_kernel_spmd as run

    def laid_out(name, *axes):
        a = np.asarray(inputs[name])
        return np.ascontiguousarray(a.transpose(axes) if axes else a)

    arrays = {
        "x": laid_out("x"), "ctxT": laid_out("ctx_1024", 0, 2, 1), "mask": laid_out("fside_Bx1xSxS2_0"),
        "wqT": laid_out("L0_xattn_Wq", 1, 0), "wkT": laid_out("L0_xattn_Wk", 1, 0),
        "wvT": laid_out("L0_xattn_Wv", 1, 0), "woT": laid_out("L0_xattn_Wo", 1, 0),
        "gate_wT": laid_out("L0_ffn_gate_w", 1, 0), "gate_b": laid_out("L0_ffn_gate_b"),
        "w13T": laid_out("L0_ffn_w13", 0, 2, 1), "w2T": laid_out("L0_ffn_w2", 0, 2, 1),
        "w13_sT": laid_out("L0_ffn_w13_s", 1, 0), "w2_sT": laid_out("L0_ffn_w2_s", 1, 0),
    }
    n_exp, tiles = arrays["gate_wT"].shape[1], arrays["x"].shape[1] // P
    sel = np.zeros((P, n_exp, P), np.float32)
    for e in range(n_exp):
        sel[[e, n_exp + e], e, :] = 1.0
    arrays["ident"] = np.eye(P, dtype=np.float32)
    arrays["sel"] = sel
    arrays["iota"] = np.ascontiguousarray(np.broadcast_to(np.arange(n_exp, dtype=np.float32), (P, tiles, TOPK, n_exp)))

    nc = bacc.Bacc("TRN2", target_bir_lowering=False, num_devices=1)
    ins = {n: nc.dram_tensor(f"in_{n}", a.shape, mybir.dt.from_np(a.dtype), kind="ExternalInput").ap()
           for n, a in arrays.items()}
    out = nc.dram_tensor("out", arrays["x"].shape, F32, kind="ExternalOutput").ap()
    program(nc, ins, out)
    r = run(nc, [{f"in_{n}": a for n, a in arrays.items()}], core_ids=[0])
    return r.results[0]["out"]
```

```python
from contextlib import ExitStack

import concourse.bass as bass
from concourse import mybir

F32 = mybir.dt.float32
F32R = mybir.dt.float32r
U32 = mybir.dt.uint32
ALU = mybir.AluOpType
ACT = mybir.ActivationFunctionType
AXX = mybir.AxisListType.X

P = 128
EPS = 1e-5
TOPK = 4
ROUTE_SCALE = 2.5
BIG = 3.0e38
DMA = 16


class Ring:

    def __init__(self, make_tensor, make_sem, name, size, shape, dt):
        self.tiles = [make_tensor(f"{name}{i}", shape, dt) for i in range(size)]
        self.sems = [make_sem(f"s_{name}{i}") for i in range(size)]
        self.size = size

    def tile(self, n):
        return self.tiles[n % self.size]

    def sem(self, n):
        return self.sems[n % self.size]

    def wait(self, eng, n):
        eng.wait_ge(self.sem(n), DMA * (n // self.size + 1))


def f32(ap):
    return ap.bitcast(F32)


def split_products(eng, out, left, right, first=True, last=True):
    eng.matmul(out, left[0], right[0], start=first, stop=False)
    eng.matmul(out, left[0], right[1], start=False, stop=False)
    return eng.matmul(out, left[1], right[0], start=False, stop=last)


def attention_phase(nc, ident_dram, x, ctxT, mask, wqT, wkT, wvT, woT, x2):
    B, S, D = x.shape
    INNER = wqT.shape[1]
    DH = 64
    H = INNER // DH
    NT = S // P
    NK = D // P
    NP = H // 2
    NE = INNER // P
    G = B * H

    EXP_LAG, T_LAG, PV_LAG = 1, 3, 4
    E_RING, PT_RING, QK_RING = 5, 3, 3
    QK_LEAD = QK_RING - 1
    CM_STEP, CS_STEP, WO_STEP, ST_STEP = 1, 3, PV_LAG, PV_LAG + 1
    LN_STEP, XN_STEP, XT_STEP, V_STEPS = 5, 6, 9, (7, 11, 13, 15)

    with ExitStack() as ctx:
        def sb(name, shape, dt=F32):
            return ctx.enter_context(nc.sbuf_tensor(name, shape, dt))

        def sem(name):
            return ctx.enter_context(nc.semaphore(name))

        def pair_of(name, shape):
            return sb(name + "_hi", shape, F32R), sb(name + "_lo", shape, F32R)

        wq, wk, wv = (pair_of(n, [P, NK, INNER]) for n in ("wq", "wk", "wv"))
        wo = pair_of("wo", [P, NE, D])
        CW = NT * S
        chunks = [(w[k * P:(k + 1) * P, c:c + CW], [part[:, k, c:c + CW] for part in parts])
                  for w, parts in ((wkT, wk), (wqT, wq), (wvT, wv)) for k in range(NK) for c in range(0, INNER, CW)]
        EC = CW // D
        chunks += [(woT[c * P:(c + EC) * P, :].rearrange("(k p) n -> p k n", p=P), [part[:, c:c + EC, :] for part in wo])
                   for c in range(0, NE, EC)]
        W_K = NK * INNER // CW
        W_Q, W_V, W_O = 2 * W_K, 3 * W_K, len(chunks)

        def staged(i):
            part = chunks[i][1][0]
            return E[i % E_RING][:, :, :].rearrange("p a b -> p (a b)") if len(part.shape) == 2 else E[i % E_RING][:, :, :]

        ident = sb("ident", [P, P])
        x_in = Ring(sb, sem, "x_in", 3, [P, NT, D], F32)
        c_in = Ring(sb, sem, "c_in", 2, [P, NK, S], F32)
        m_in = Ring(sb, sem, "m_in", 2, [P, NT, S], F32)
        s_x2out = [sem(f"s_x2out{i}") for i in range(x_in.size)]
        xn = sb("xn", [P, NT, D])
        xnT = [pair_of(f"xnT{i}", [P, NK, S]) for i in range(2)]
        cT = [pair_of(f"cT{i}", [P, NK, S]) for i in range(2)]
        V = [pair_of(f"V{i}", [P, NT, NP, 3, DH]) for i in range(2)]
        att = pair_of("att", [P, NE, S])
        q_st = [sb(f"q_st{i}", [P, 2, S], F32R) for i in range(QK_RING)]
        k_st = [sb(f"k_st{i}", [P, 2, 2, S], F32R) for i in range(QK_RING)]
        s_kdup = [sem(f"s_kdup{i}") for i in range(QK_RING)]
        E = [sb(f"E{i}", [P, NT, S]) for i in range(E_RING)]
        PT = [pair_of(f"PT{i}", [P, NT, S]) for i in range(PT_RING)]
        negmax = sb("negmax", [P, E_RING, NT])
        rowsum = sb("rowsum", [P, E_RING, NT])
        rinv = sb("rinv", [P, E_RING, NT])
        st6 = sb("st6", [P, NT, 6])
        mv = sb("mv", [P, NT, 2])
        veps = sb("veps", [P, NT])
        rstd = sb("rstd", [P, NT])
        mhalf = sb("mhalf", [P, NT])

        pj = [ctx.enter_context(nc.psum_tensor(f"pj{i}", [P, 512], F32)) for i in range(2)]
        pS = [ctx.enter_context(nc.psum_tensor(f"pS{i}", [P, NT, S], F32)) for i in range(2)]
        pT = [ctx.enter_context(nc.psum_tensor(f"pT{i}", [P, NT, S], F32)) for i in range(2)]
        pV = [ctx.enter_context(nc.psum_tensor(f"pV{i}", [P, 512], F32)) for i in range(2)]

        s_ident, s_whi, s_wlo = sem("s_ident"), sem("s_whi"), sem("s_wlo")
        s_stage = [sem(f"s_stage{i}") for i in range(E_RING)]
        s_const = sem("s_const")
        s_pj, s_hi, s_pjfree = sem("s_pj"), sem("s_hi"), sem("s_pjfree")
        s_S, s_T, s_PV = sem("s_S"), sem("s_T"), sem("s_PV")
        s_max, s_exp, s_rinv, s_norm = sem("s_max"), sem("s_exp"), sem("s_rinv"), sem("s_norm")
        s_pthi, s_ptlo, s_atthi, s_attlo = sem("s_pthi"), sem("s_ptlo"), sem("s_atthi"), sem("s_attlo")
        s_bn, s_agg, s_veps, s_rstd, s_xn = sem("s_bn"), sem("s_agg"), sem("s_veps"), sem("s_rstd"), sem("s_xn")
        s_chi, s_clo = sem("s_chi"), sem("s_clo")

        uses, number = {}, {}

        def use(step, what):
            number[what] = len(number)
            uses.setdefault(step, []).append(what)

        PRE = -1
        use(PRE, ("xT", 0))
        for pair in range(QK_LEAD):
            use(PRE, ("k", pair))
            use(PRE, ("q", pair))
        for g in range(G + WO_STEP + NT):
            b, h = divmod(g, H)
            if g < G and h % 2 == 0 and g // 2 + QK_LEAD < G // 2:
                use(g, ("k", g // 2 + QK_LEAD))
                use(g, ("q", g // 2 + QK_LEAD))
            if g < 2 * NT:
                use(g, ("v", 0, g))
            if WO_STEP <= h < WO_STEP + NT and b >= 1:
                use(g, ("wo", b - 1, h - WO_STEP))
            if h == XT_STEP and b + 1 < B:
                use(g, ("xT", b + 1))
            if h in V_STEPS and b + 1 < B:
                use(g, ("v", b + 1, V_STEPS.index(h)))
        steps = range(PRE, max(uses) + 1)

        WO_LAST = NT - 1
        assert len(V_STEPS) == 2 * NT and max(V_STEPS) < H and WO_STEP + NT - 1 == ST_STEP

        def qk_buf(pair):
            return pair % QK_RING

        block = ctx.enter_context(nc.Block())

        @block.sync
        def _(sp):
            sp.dma_start(ident[:, :], ident_dram).then_inc(s_ident, DMA)

            def load_x(n):
                if n < B:
                    if n >= x_in.size:
                        sp.wait_ge(s_x2out[n % x_in.size], DMA * (n // x_in.size))
                    sp.dma_start(x_in.tile(n)[:, :, :], x[n].rearrange("(t p) d -> p t d", p=P)).then_inc(x_in.sem(n), DMA)

            def load_context(n):
                if n < B:
                    if n >= c_in.size:
                        sp.wait_ge(s_clo, n - c_in.size + 1)
                    sp.dma_start(c_in.tile(n)[:, :, :], ctxT[n].rearrange("(k p) s -> p k s", p=P)).then_inc(c_in.sem(n), DMA)

            def load_mask(n):
                if n < B:
                    if n >= 2:
                        sp.wait_ge(s_max, H * (n - 1))
                    sp.dma_start(m_in.tile(n)[:, :, :], mask[n, 0].rearrange("(t p) s -> p t s", p=P)).then_inc(m_in.sem(n), DMA)

            load_x(0)
            load_context(0)
            for i, (w, parts) in enumerate(chunks):
                if i >= E_RING:
                    sp.wait_ge(s_wlo, i - E_RING + 1)
                if i == W_Q:
                    load_mask(0)
                sp.dma_start(staged(i), w).then_inc(s_stage[i % E_RING], DMA)
            for n in range(1, x_in.size):
                load_x(n)

            def copy_keys(pair):
                sp.wait_ge(s_pjfree, number[("k", pair)] + 1)
                st, s_copied = k_st[qk_buf(pair)], s_kdup[qk_buf(pair)]
                sp.dma_start(f32(st[DH:P, 0, :, :]), f32(st[0:DH, 0, :, :])).then_inc(s_copied, DMA)
                sp.dma_start(f32(st[0:DH, 1, :, :]), f32(st[DH:P, 1, :, :])).then_inc(s_copied, DMA)

            def store(b):
                sp.wait_ge(s_pjfree, number[("wo", b, WO_LAST)] + 1)
                sp.dma_start(x2[b].rearrange("(t p) d -> p t d", p=P), x_in.tile(b)[:, :, :]).then_inc(
                    s_x2out[b % x_in.size], DMA)

            for g in steps:
                b, h = divmod(g, H)
                for what in uses.get(g, ()):
                    if what[0] == "k":
                        copy_keys(what[1])
                if h == CM_STEP:
                    load_context(b + 1)
                    load_mask(b + 1)
                if h == ST_STEP and b:
                    store(b - 1)
                    load_x(b - 1 + x_in.size)
            for b in range(max(0, B - x_in.size), B):
                sp.wait_ge(s_x2out[b % x_in.size], DMA * (b // x_in.size + 1))

        @block.gpsimd
        def _(pool):
            pool.memset(mhalf[:, :], -0.5).then_inc(s_const, 1)
            for pair in V:
                for part in pair:
                    pool.memset(f32(part[:, :, :, 1, :]), 0.0).then_inc(s_const, 1)
            pool.wait_ge(s_const, 5)

            def split_context(b):
                if b >= 2:
                    pool.wait_ge(s_pj, max(number[("k", b * NP - NP - 1)], number[("v", b - 2, 2 * NT - 1)]) + 1)
                c_in.wait(pool, b)
                hi, lo = cT[b % 2]
                pool.tensor_copy(hi[:, :, :], c_in.tile(b)[:, :, :]).then_inc(s_chi, 1)
                pool.wait_ge(s_chi, b + 1)
                pool.tensor_tensor(lo[:, :, :], c_in.tile(b)[:, :, :], f32(hi[:, :, :]), ALU.subtract).then_inc(s_clo, 1)

            def inverse_std(b):
                pool.wait_ge(s_veps, b + 1)
                pool.tensor_tensor(rstd[:, :], veps[:, :], mhalf[:, :], ALU.pow).then_inc(s_rstd, 1)

            inverse_std(0)
            split_context(0)
            for g in range(G):
                b, h = divmod(g, H)
                pool.wait_ge(s_exp, g + 1)
                pool.wait_ge(s_rinv, g + 1)
                e, r = E[g % E_RING], g % E_RING
                for t in range(NT):
                    last = pool.tensor_scalar(e[:, t, :], e[:, t, :], rinv[:, r, t:t + 1], 1.0, ALU.mult, ALU.mult)
                last.then_inc(s_norm, 1)
                if h == CS_STEP and b + 1 < B:
                    split_context(b + 1)
                if h == LN_STEP and b + 1 < B:
                    inverse_std(b + 1)

        @block.tensor
        def _(pe):
            def bank(what):
                n = number[what]
                if n >= 2:
                    pe.wait_ge(s_pjfree, n - 1)
                return pj[n % 2]

            def fill(what):
                kind, n = what[0], what[1]
                ps = bank(what)
                if kind == "xT":
                    pe.wait_ge(s_xn, n + 1)
                    for t in range(NT):
                        for k in range(NK):
                            last = pe.transpose(ps[:, k * S + t * P:k * S + (t + 1) * P],
                                                xn[:, t, k * P:(k + 1) * P], ident[:, :])
                elif kind == "v":
                    pe.wait_ge(s_clo, n + 1)
                    if n == 0:
                        pe.wait_ge(s_wlo, W_V)
                    t, half = divmod(what[2], 2)
                    for k in range(NK):
                        last = split_products(
                            pe, ps[:, :], [c[:, k, t * P:(t + 1) * P] for c in cT[n % 2]],
                            [w[:, k, half * 512:(half + 1) * 512] for w in wv], k == 0, k == NK - 1)
                elif kind == "q":
                    b, j = divmod(n, NP)
                    if n == 0:
                        pe.wait_ge(s_wlo, W_Q)
                    pe.wait_ge(s_pjfree, number[("xT", b)] + 1)
                    for k in range(NK):
                        last = split_products(
                            pe, ps[:, 0:S], [w[:, k, j * P:(j + 1) * P] for w in wq],
                            [a[:, k, :] for a in xnT[b % 2]], k == 0, k == NK - 1)
                elif kind == "k":
                    b, j = divmod(n, NP)
                    pe.wait_ge(s_clo, b + 1)
                    for k in range(NK):
                        last = split_products(
                            pe, ps[:, 0:S], [w[:, k, j * P:(j + 1) * P] for w in wk],
                            [c[:, k, :] for c in cT[b % 2]], k == 0, k == NK - 1)
                else:
                    if n == 0:
                        pe.wait_ge(s_wlo, W_O)
                    pe.wait_ge(s_attlo, (n + 1) * NP)
                    t = what[2]
                    for k in range(NE):
                        last = split_products(pe, ps[:, 0:D], [a[:, k, t * P:(t + 1) * P] for a in att],
                                              [w[:, k, :] for w in wo], k == 0, k == NE - 1)
                last.then_inc(s_pj, 1)

            def scores(g):
                pair, a = divmod(g, 2)
                if a == 0:
                    pe.wait_ge(s_pjfree, number[("q", pair)] + 1)
                    pe.wait_ge(s_kdup[qk_buf(pair)], 2 * DMA * (pair // QK_RING + 1))
                if g >= 2:
                    pe.wait_ge(s_max, g - 1)
                q = q_st[qk_buf(pair)]
                for t in range(NT):
                    left = q[:, a, t * P:(t + 1) * P]
                    pe.matmul(pS[g % 2][:, t, :], left, k_st[qk_buf(pair)][:, a, 0, :], start=True, stop=False)
                    last = pe.matmul(pS[g % 2][:, t, :], left, k_st[qk_buf(pair)][:, a, 1, :], start=False, stop=True)
                last.then_inc(s_S, 1)

            def transpose_probs(g):
                pe.wait_ge(s_norm, g + 1)
                if g >= 2:
                    pe.wait_ge(s_ptlo, g - 1)
                e = E[g % E_RING]
                for t in range(NT):
                    for k in range(NT):
                        last = pe.transpose(pT[g % 2][:, k, t * P:(t + 1) * P], e[:, t, k * P:(k + 1) * P], ident[:, :])
                last.then_inc(s_T, 1)

            def values(g):
                pair, a = divmod(g, 2)
                b, j = divmod(pair, NP)
                pe.wait_ge(s_ptlo, g + 1)
                if j == 0 and a == 0:
                    pe.wait_ge(s_pjfree, number[("v", b, 2 * NT - 1)] + 1)
                if a == 0 and pair >= 2:
                    pe.wait_ge(s_attlo, pair - 1)
                for k in range(NT):
                    last = split_products(
                        pe, pV[pair % 2][:, 0:S], [v[:, k, j, a:a + 2, :] for v in V[b % 2]],
                        [p[:, k, :] for p in PT[g % PT_RING]], a == 0 and k == 0, a == 1 and k == NT - 1)
                last.then_inc(s_PV, 1)

            pe.wait_ge(s_ident, DMA)
            pe.wait_ge(s_wlo, W_K)
            pe.wait_ge(s_const, 5)
            for g in steps:
                if 0 <= g < G:
                    scores(g)
                todo = uses.get(g, ())
                for what in todo[:1]:
                    fill(what)
                if 0 <= g - T_LAG < G:
                    transpose_probs(g - T_LAG)
                for what in todo[1:2]:
                    fill(what)
                if 0 <= g - PV_LAG < G:
                    values(g - PV_LAG)
                for what in todo[2:]:
                    fill(what)

        @block.scalar
        def _(act):
            def weight_hi(i):
                act.wait_ge(s_stage[i % E_RING], DMA * (i // E_RING + 1))
                act.activation(chunks[i][1][0], staged(i), ACT.Copy).then_inc(s_whi, 1)

            def hi_part(what):
                kind, n = what[0], what[1]
                if kind == "wo":
                    return
                act.wait_ge(s_pj, number[what] + 1)
                ps = pj[number[what] % 2]
                if kind == "xT":
                    if n >= 2:
                        act.wait_ge(s_pj, number[("q", (n - 1) * NP - 1)] + 1)
                    last = act.activation(xnT[n % 2][0][:, :, :], ps[:, :].rearrange("p (k s) -> p k s", k=NK), ACT.Copy)
                elif kind == "v":
                    if n >= 2 and what[2] == 0:
                        act.wait_ge(s_PV, (n - 1) * H)
                    t, half = divmod(what[2], 2)
                    j = half * NP // 2
                    last = act.activation(V[n % 2][0][:, t, j:j + NP // 2, 0:3:2, :],
                                          ps[:, :].rearrange("p (j a d) -> p j a d", a=2, d=DH), ACT.Copy)
                else:
                    if n >= QK_RING:
                        act.wait_ge(s_S, 2 * (n - QK_RING + 1))
                    st = q_st[qk_buf(n)] if kind == "q" else k_st[qk_buf(n)][:, :, 0, :]
                    for a in range(2):
                        at = slice(a * DH, (a + 1) * DH)
                        last = act.activation(st[at, a, :], ps[at, 0:S], ACT.Copy)
                last.then_inc(s_hi, 1)

            for i in range(len(chunks)):
                weight_hi(i)
            for g in steps:
                n = g - EXP_LAG
                if 0 <= n < G:
                    act.wait_ge(s_max, n + 1)
                    if n >= E_RING:
                        act.wait_ge(s_rinv, n - E_RING + 1)
                    r = n % E_RING
                    for t in range(NT):
                        last = act.activation(E[r][:, t, :], E[r][:, t, :], ACT.Exp, bias=negmax[:, r, t:t + 1],
                                              scale=-1.0, accum_out=rowsum[:, r, t:t + 1])
                    last.then_inc(s_exp, 1)
                todo = uses.get(g, ())
                for what in todo[:1]:
                    hi_part(what)
                if 0 <= g - T_LAG < G:
                    n = g - T_LAG
                    act.wait_ge(s_T, n + 1)
                    if n >= PT_RING:
                        act.wait_ge(s_PV, n - PT_RING + 1)
                    act.activation(PT[n % PT_RING][0][:, :, :], pT[n % 2][:, :, :], ACT.Copy).then_inc(s_pthi, 1)
                for what in todo[1:2]:
                    hi_part(what)
                n = g - PV_LAG
                if 0 <= n < G and n % 2:
                    pair = n // 2
                    b, j = divmod(pair, NP)
                    act.wait_ge(s_PV, n + 1)
                    if b and j == 0:
                        act.wait_ge(s_pj, number[("wo", b - 1, WO_LAST)] + 1)
                    act.activation(att[0][:, j, :], pV[pair % 2][:, 0:S], ACT.Copy).then_inc(s_atthi, 1)
                for what in todo[2:]:
                    hi_part(what)

        @block.vector
        def _(dve):
            his = [0]

            def normalise(b):
                x_in.wait(dve, b)
                xb = x_in.tile(b)
                for t in range(NT):
                    last = dve.bn_stats(st6[:, t, :], xb[:, t, :])
                last.then_inc(s_bn, 1)
                dve.wait_ge(s_bn, b + 1)
                for t in range(NT):
                    last = dve.bn_aggr(mv[:, t, :], st6[:, t, :])
                last.then_inc(s_agg, 1)
                dve.wait_ge(s_agg, b + 1)
                dve.tensor_scalar(veps[:, :], mv[:, :, 1], EPS, None, ALU.add).then_inc(s_veps, 1)

            def apply_norm(b):
                dve.wait_ge(s_rstd, b + 1)
                if b:
                    dve.wait_ge(s_pj, number[("xT", b - 1)] + 1)
                for t in range(NT):
                    last = dve.tensor_scalar(xn[:, t, :], x_in.tile(b)[:, t, :], mv[:, t, 0:1], rstd[:, t:t + 1],
                                             ALU.subtract, ALU.mult)
                last.then_inc(s_xn, 1)

            def lo_part(what):
                kind, n = what[0], what[1]
                ps = pj[number[what] % 2]
                if kind == "wo":
                    dve.wait_ge(s_pj, number[what] + 1)
                    xt = x_in.tile(n)[:, what[2], :]
                    last = dve.tensor_tensor(xt, ps[:, 0:D], xt, ALU.add)
                    last.then_inc(s_pjfree, 1)
                    return
                his[0] += 1
                dve.wait_ge(s_hi, his[0])
                if kind == "xT":
                    hi, lo = xnT[n % 2]
                    last = dve.tensor_tensor(lo[:, :, :], ps[:, :].rearrange("p (k s) -> p k s", k=NK), f32(hi[:, :, :]), ALU.subtract)
                elif kind == "v":
                    t, half = divmod(what[2], 2)
                    j = half * NP // 2
                    hi, lo = (v[:, t, j:j + NP // 2, 0:3:2, :] for v in V[n % 2])
                    last = dve.tensor_tensor(lo, ps[:, :].rearrange("p (j a d) -> p j a d", a=2, d=DH), f32(hi), ALU.subtract)
                elif kind == "q":
                    q = q_st[qk_buf(n)]
                    dve.tensor_tensor(q[DH:P, 0, :], ps[0:DH, 0:S], f32(q[0:DH, 0, :]), ALU.subtract)
                    last = dve.tensor_tensor(q[0:DH, 1, :], ps[DH:P, 0:S], f32(q[DH:P, 1, :]), ALU.subtract)
                else:
                    st = k_st[qk_buf(n)]
                    for a in range(2):
                        at = slice(a * DH, (a + 1) * DH)
                        last = dve.tensor_tensor(st[at, a, 1, :], ps[at, 0:S], f32(st[at, a, 0, :]), ALU.subtract)
                last.then_inc(s_pjfree, 1)

            def inverse_sums(g):
                r = g % E_RING
                dve.wait_ge(s_exp, g + 1)
                if g >= E_RING:
                    dve.wait_ge(s_norm, g - E_RING + 1)
                dve.reciprocal(rinv[:, r, :], rowsum[:, r, :]).then_inc(s_rinv, 1)

            normalise(0)
            apply_norm(0)
            for i, (_, (hi, lo)) in enumerate(chunks):
                dve.wait_ge(s_whi, i + 1)
                dve.tensor_tensor(lo, staged(i), f32(hi), ALU.subtract).then_inc(s_wlo, 1)
            for g in steps:
                b, h = divmod(g, H)
                if 0 <= g < G:
                    r = g % E_RING
                    dve.wait_ge(s_S, g + 1)
                    if h == 0:
                        m_in.wait(dve, b)
                    if g >= E_RING:
                        dve.wait_ge(s_T, g - E_RING + 1)
                    for t in range(NT):
                        last = dve.tensor_tensor_reduce(
                            out=E[r][:, t, :], in0=pS[g % 2][:, t, :], in1=m_in.tile(b)[:, t, :], scale=-1.0,
                            scalar=BIG, op0=ALU.add, op1=ALU.min, accum_out=negmax[:, r, t:t + 1])
                    last.then_inc(s_max, 1)
                if 0 <= g - EXP_LAG < G:
                    inverse_sums(g - EXP_LAG)
                todo = uses.get(g, ())
                for what in todo[:1]:
                    lo_part(what)
                if 0 <= g - T_LAG < G:
                    n = g - T_LAG
                    dve.wait_ge(s_pthi, n + 1)
                    hi, lo = PT[n % PT_RING]
                    dve.tensor_tensor(lo[:, :, :], pT[n % 2][:, :, :], f32(hi[:, :, :]), ALU.subtract).then_inc(s_ptlo, 1)
                for what in todo[1:2]:
                    lo_part(what)
                n = g - PV_LAG
                if 0 <= n < G and n % 2:
                    pair = n // 2
                    j = pair % NP
                    dve.wait_ge(s_atthi, pair + 1)
                    dve.tensor_tensor(att[1][:, j, :], pV[pair % 2][:, 0:S], f32(att[0][:, j, :]), ALU.subtract).then_inc(s_attlo, 1)
                for what in todo[2:]:
                    lo_part(what)
                if 0 <= g < G and b + 1 < B:
                    if h == LN_STEP:
                        normalise(b + 1)
                    if h == XN_STEP:
                        apply_norm(b + 1)


def expert_phase(nc, ident_dram, sel_dram, iota_dram, x2, gate_wT, gate_b, w13T, w2T, w13_sT, w2_sT, out):
    B, S, D = x2.shape
    N_EXP = gate_wT.shape[1]
    INTER = w2T.shape[1]
    NX = N_EXP + 1
    NT, NK = S // P, D // P
    ND = N_EXP * 2

    with ExitStack() as ctx:
        def sb(name, shape, dt=F32):
            return ctx.enter_context(nc.sbuf_tensor(name, shape, dt))

        def sem(name):
            return ctx.enter_context(nc.semaphore(name))

        def pair_of(name, shape):
            return sb(name + "_hi", shape, F32R), sb(name + "_lo", shape, F32R)

        w13 = pair_of("w13", [P, NX, NK, 2 * INTER])
        w2 = pair_of("w2", [P, NX, D])
        gw = pair_of("gw", [P, NK, N_EXP])
        stage = Ring(sb, sem, "wstage", 4, [P, NK * 2 * INTER + D], F32)
        gw_raw = sb("gw_raw", [P, NK, N_EXP])
        gb = sb("gb", [P, NT, N_EXP])
        ident = sb("ident2", [P, P])
        sel_raw = sb("sel_raw", [P, N_EXP, P])
        sel = sb("sel", [P, N_EXP, P], F32R)
        iota = sb("iota", [P, NT, TOPK, N_EXP])
        x_in = Ring(sb, sem, "y_in", 3, [P, NT, D], F32)
        s_out = [sem(f"s_out{i}") for i in range(3)]
        xn = sb("xn2", [P, NT, D])
        xnT = [pair_of(f"xnT2_{i}", [P, NK, S]) for i in range(2)]
        st6, mv = sb("st6b", [P, NT, 6]), sb("mvb", [P, NT, 2])
        veps, rstd, mhalf = sb("vepsb", [P, NT]), sb("rstdb", [P, NT]), sb("mhalfb", [P, NT])
        lgT = sb("lgT", [N_EXP, S])
        sc, bi = sb("sc", [P, NT, N_EXP]), sb("bi", [P, NT, N_EXP])
        top, topi = sb("top", [P, NT, 8]), sb("topi", [P, NT, 8], U32)
        topf = sb("topf", [P, NT, TOPK])
        onehot = sb("onehot", [P, NT, TOPK, N_EXP])
        chosen, wsum, wrec = sb("chosen", [P, NT, N_EXP]), sb("wsum", [P, NT]), sb("wrec", [P, NT])
        wch, comb = sb("wch", [P, NT, N_EXP]), sb("comb", [P, NT, N_EXP])
        csplit = sb("csplit", [P, NT, ND])
        chi = sb("chi", [P, NT, N_EXP], F32R)
        combT = [sb(f"combT{i}", [P, S], F32R) for i in range(2)]
        sig = [sb(f"sig{i}", [P, S]) for i in range(2)]
        hid = [sb(f"hid{i}", [P, S]) for i in range(2)]
        hsp = [pair_of(f"hsp{i}", [P, S]) for i in range(3)]

        pGU = [ctx.enter_context(nc.psum_tensor(f"pGU{i}", [P, 2, S], F32)) for i in range(2)]
        pC = [ctx.enter_context(nc.psum_tensor(f"pC{i}", [P, 512], F32)) for i in range(2)]
        pY = [ctx.enter_context(nc.psum_tensor(f"pY{i}", [P, 512], F32)) for i in range(NT)]
        pM = [ctx.enter_context(nc.psum_tensor(f"pM{i}", [P, 512], F32)) for i in range(2)]

        s_ld, s_const, s_cst2 = sem("t_ld"), sem("t_const"), sem("t_const2")
        s_whi, s_wlo = sem("t_whi"), sem("t_wlo")
        s_veps, s_rstd, s_xn = sem("t_veps"), sem("t_rstd"), sem("t_xn")
        s_xT, s_xhi, s_xlo = sem("t_xT"), sem("t_xhi"), sem("t_xlo")
        s_lg, s_lgc, s_lgt, s_sc = sem("t_lg"), sem("t_lgc"), sem("t_lgt"), sem("t_sc")
        s_comb, s_cT, s_combT = sem("t_comb"), sem("t_cT"), sem("t_combT")
        s_GU, s_C, s_sig, s_hid, s_hhi, s_hlo, s_y, s_yout = (
            sem(n) for n in ("t_GU", "t_C", "t_sig", "t_hid", "t_hhi", "t_hlo", "t_y", "t_yout"))
        s_chain = sem("t_chain")

        XI = [(b, e) for b in range(B) for e in range(NX)]
        N = len(XI)
        W2_LAG = 2
        LN_AT, XN_AT, XT_AT, LG_AT, LGT_AT, RT_AT = 2, 4, 5, 7, 8, 9
        CT_AT = RT_AT + 6

        block = ctx.enter_context(nc.Block())

        @block.sync
        def _(sp):
            sp.dma_start(ident[:, :], ident_dram).then_inc(s_ld, DMA)
            sp.dma_start(sel_raw[:, :, :], sel_dram).then_inc(s_ld, DMA)
            sp.dma_start(iota[:, :, :, :], iota_dram).then_inc(s_ld, DMA)
            sp.dma_start(gw_raw[:, :, :], gate_wT.rearrange("(k p) e -> p k e", p=P)).then_inc(s_ld, DMA)
            for t in range(NT):
                sp.dma_start(gb[:, t, :], gate_b.partition_broadcast(P)).then_inc(s_ld, DMA)

            def load(n):
                if n < B:
                    if n >= 3:
                        sp.wait_ge(s_out[n % 3], DMA * (n // 3))
                    sp.dma_start(x_in.tile(n)[:, :, :], x2[n].rearrange("(t p) d -> p t d", p=P)).then_inc(x_in.sem(n), DMA)

            load(0)
            load(1)
            W13 = NK * 2 * INTER
            for e in range(NX):
                if e >= stage.size:
                    sp.wait_ge(s_wlo, e - stage.size + 1)
                a = w13T[e] if e < N_EXP else w13_sT
                c = w2T[e] if e < N_EXP else w2_sT
                sp.dma_start(stage.tile(e)[:, 0:W13].rearrange("p (k n) -> p k n", k=NK),
                             a.rearrange("(k p) n -> p k n", p=P)).then_inc(stage.sem(e), DMA)
                sp.dma_start(stage.tile(e)[:, W13:W13 + D], c).then_inc(stage.sem(e), DMA)
            load(2)
            for b in range(B):
                sp.wait_ge(s_yout, b + 1)
                sp.dma_start(out[b].rearrange("(t p) d -> p t d", p=P), x_in.tile(b)[:, :, :]).then_inc(s_out[b % 3], DMA)
                load(b + 3)
            for b in range(max(0, B - 3), B):
                sp.wait_ge(s_out[b % 3], DMA * (b // 3 + 1))

        def weights_here(eng, e):
            eng.wait_ge(stage.sem(e), 2 * DMA * (e // stage.size + 1))

        def staged(e):
            W13 = NK * 2 * INTER
            t = stage.tile(e)
            return t[:, 0:W13].rearrange("p (k n) -> p k n", k=NK), t[:, W13:W13 + D]

        @block.gpsimd
        def _(pool):
            pool.memset(mhalf[:, :], -0.5).then_inc(s_const, 1)
            for c in combT:
                pool.memset(f32(c[:, :]), 0.0).then_inc(s_const, 1)
            pool.wait_ge(s_const, 3)

            def inverse_std(b):
                pool.wait_ge(s_veps, b + 1)
                pool.tensor_tensor(rstd[:, :], veps[:, :], mhalf[:, :], ALU.pow).then_inc(s_rstd, 1)

            inverse_std(0)
            for i, (b, e) in enumerate(XI):
                pool.wait_ge(s_hhi, i + 1)
                hi, lo = hsp[i % 3]
                if i >= 3:
                    pool.wait_ge(s_y, i - 2)
                pool.tensor_tensor(lo[:, :], hid[i % 2][:, :], f32(hi[:, :]), ALU.subtract).then_inc(s_hlo, 1)
                if e == LN_AT and b + 1 < B:
                    inverse_std(b + 1)

        @block.tensor
        def _(pe):
            def transposed_x(b):
                pe.wait_ge(s_xn, b + 1)
                for t in range(NT):
                    for k in range(NK):
                        last = pe.transpose(pM[0][:, k * S + t * P:k * S + (t + 1) * P],
                                            xn[:, t, k * P:(k + 1) * P], ident[:, :])
                last.then_inc(s_xT, 1)

            def logits(b):
                pe.wait_ge(s_xlo, b + 1)
                if b:
                    pe.wait_ge(s_combT, b)
                for k in range(NK):
                    last = split_products(pe, pM[1][0:N_EXP, 0:S], [g[:, k, :] for g in gw],
                                          [a[:, k, :] for a in xnT[b % 2]], k == 0, k == NK - 1)
                last.then_inc(s_lg, 1)

            def logits_by_token(b):
                pe.wait_ge(s_lgc, b + 1)
                for t in range(NT):
                    last = pe.transpose(pM[1][:, t * N_EXP:(t + 1) * N_EXP], lgT[:, t * P:(t + 1) * P],
                                        ident[0:N_EXP, 0:N_EXP])
                last.then_inc(s_lgt, 1)

            def comb_by_expert(b):
                pe.wait_ge(s_comb, b + 1)
                for t in range(NT):
                    last = pe.transpose(pM[1][0:ND, t * P:(t + 1) * P], csplit[:, t, :], ident[:, :])
                last.then_inc(s_cT, 1)

            prepare = {XT_AT: transposed_x, LG_AT: logits, LGT_AT: logits_by_token, CT_AT: comb_by_expert}
            pe.wait_ge(s_ld, 6 * DMA)
            pe.wait_ge(s_cst2, 3)
            for at in sorted(prepare):
                prepare[at](0)
            for i in range(N + W2_LAG):
                if i < N:
                    b, e = XI[i]
                    if b == 0:
                        pe.wait_ge(s_wlo, e + 1)
                    if i >= 2:
                        pe.wait_ge(s_hid, i - 1)
                    for m in range(2):
                        for k in range(NK):
                            last = split_products(pe, pGU[i % 2][:, m, :],
                                                  [w[:, e, k, m * INTER:(m + 1) * INTER] for w in w13],
                                                  [a[:, k, :] for a in xnT[b % 2]], k == 0, k == NK - 1)
                    last.then_inc(s_GU, 1)
                    if e < N_EXP:
                        if e == 0:
                            pe.wait_ge(s_combT, b + 1)
                        pe.matmul(pC[i % 2][:, 0:S], sel[:, e, :], combT[b % 2][:, :], start=True, stop=True).then_inc(s_C, 1)
                    if e in prepare and b + 1 < B:
                        prepare[e](b + 1)
                if i >= W2_LAG:
                    n = i - W2_LAG
                    b, e = XI[n]
                    pe.wait_ge(s_hlo, n + 1)
                    if e == 0 and b:
                        pe.wait_ge(s_yout, b)
                    for t in range(NT):
                        last = split_products(pe, pY[t][:, 0:D], [h[:, t * P:(t + 1) * P] for h in hsp[n % 3]],
                                              [w[:, e, :] for w in w2], e == 0, e == NX - 1)
                    last.then_inc(s_y, 1)

        @block.scalar
        def _(act):
            act.wait_ge(s_ld, 6 * DMA)
            act.activation(gw[0][:, :, :], gw_raw[:, :, :], ACT.Copy).then_inc(s_cst2, 1)
            act.activation(sel[:, :, :], sel_raw[:, :, :], ACT.Copy).then_inc(s_cst2, 1)

            def x_hi(b):
                act.wait_ge(s_xT, b + 1)
                if b >= 2:
                    act.wait_ge(s_GU, (b - 1) * NX)
                act.activation(xnT[b % 2][0][:, :, :], pM[0][:, :].rearrange("p (k s) -> p k s", k=NK), ACT.Copy).then_inc(s_xhi, 1)

            def logit_copy(b):
                act.wait_ge(s_lg, b + 1)
                act.activation(lgT[:, :], pM[1][0:N_EXP, 0:S], ACT.Copy).then_inc(s_lgc, 1)

            def gate_scores(b):
                act.wait_ge(s_lgt, b + 1)
                if b:
                    act.wait_ge(s_comb, b)
                act.activation(sc[:, :, :], pM[1][:, 0:NT * N_EXP].rearrange("p (t e) -> p t e", t=NT),
                               ACT.Sigmoid).then_inc(s_sc, 1)

            def weight_hi(e):
                weights_here(act, e)
                a, c = staged(e)
                act.activation(w13[0][:, e, :, :], a, ACT.Copy)
                act.activation(w2[0][:, e, :], c, ACT.Copy).then_inc(s_whi, 1)

            def hidden_hi(i):
                act.wait_ge(s_hid, i + 1)
                if i >= 3:
                    act.wait_ge(s_y, i - 2)
                act.activation(hsp[i % 3][0][:, :], hid[i % 2][:, :], ACT.Copy).then_inc(s_hhi, 1)

            prepare = {XT_AT: x_hi, LG_AT: logit_copy, LGT_AT: gate_scores}
            for at in sorted(prepare):
                prepare[at](0)
            weight_hi(0)
            weight_hi(1)
            for i, (b, e) in enumerate(XI):
                if b == 0 and e + 2 < NX:
                    weight_hi(e + 2)
                act.wait_ge(s_GU, i + 1)
                if i >= 2:
                    act.wait_ge(s_hid, i - 1)
                act.activation(sig[i % 2][:, :], pGU[i % 2][:, 0, :], ACT.Sigmoid).then_inc(s_sig, 1)
                if e in prepare and b + 1 < B:
                    prepare[e](b + 1)
                if i:
                    hidden_hi(i - 1)
            hidden_hi(N - 1)

        @block.vector
        def _(dve):
            chain = [0]

            def then(ins):
                chain[0] += 1
                ins.then_inc(s_chain, 1)
                dve.wait_ge(s_chain, chain[0])

            def statistics(b):
                x_in.wait(dve, b)
                xb = x_in.tile(b)
                dve.bn_stats(st6[:, 0, :], xb[:, 0, :])
                then(dve.bn_stats(st6[:, 1, :], xb[:, 1, :]))
                dve.bn_aggr(mv[:, 0, :], st6[:, 0, :])
                then(dve.bn_aggr(mv[:, 1, :], st6[:, 1, :]))
                dve.tensor_scalar(veps[:, :], mv[:, :, 1], EPS, None, ALU.add).then_inc(s_veps, 1)

            def apply_norm(b):
                dve.wait_ge(s_rstd, b + 1)
                if b:
                    dve.wait_ge(s_xT, b)
                for t in range(NT):
                    last = dve.tensor_scalar(xn[:, t, :], x_in.tile(b)[:, t, :], mv[:, t, 0:1], rstd[:, t:t + 1],
                                             ALU.subtract, ALU.mult)
                last.then_inc(s_xn, 1)

            def x_lo(b):
                dve.wait_ge(s_xhi, b + 1)
                hi, lo = xnT[b % 2]
                dve.tensor_tensor(lo[:, :, :], pM[0][:, :].rearrange("p (k s) -> p k s", k=NK), f32(hi[:, :, :]),
                                  ALU.subtract).then_inc(s_xlo, 1)

            def biased_top(b):
                dve.wait_ge(s_sc, b + 1)
                then(dve.tensor_tensor(bi[:, :, :], sc[:, :, :], gb[:, :, :], ALU.add))
                for t in range(NT):
                    last = dve.max(top[:, t, :], bi[:, t, :])
                then(last)

            def top_numbers(b):
                for t in range(NT):
                    last = dve.max_index(topi[:, t, :], top[:, t, :], bi[:, t, :])
                then(last)
                then(dve.tensor_copy(topf[:, :, :], topi[:, :, 0:TOPK]))

            def choose(b):
                then(dve.tensor_tensor(onehot[:, :, :, :], iota[:, :, :, :],
                                       topf[:, :, :].unsqueeze(3).broadcast_to([P, NT, TOPK, N_EXP]), ALU.is_equal))
                then(dve.reduce_sum(chosen[:, :, :], onehot[:, :, :, :].rearrange("p t j e -> p t e j"), AXX))

            def weigh(b):
                then(dve.tensor_tensor(wch[:, :, :], chosen[:, :, :], sc[:, :, :], ALU.mult))
                then(dve.reduce_sum(wsum[:, :], wch[:, :, :], AXX))
                then(dve.reciprocal(wrec[:, :], wsum[:, :]))
                for t in range(NT):
                    last = dve.tensor_scalar(comb[:, t, :], wch[:, t, :], wrec[:, t:t + 1], ROUTE_SCALE, ALU.mult, ALU.mult)
                then(last)

            def split_weights(b):
                then(dve.tensor_copy(chi[:, :, :], comb[:, :, :]))
                if b:
                    dve.wait_ge(s_cT, b)
                dve.tensor_copy(csplit[:, :, 0:N_EXP], f32(chi[:, :, :]))
                dve.tensor_tensor(csplit[:, :, N_EXP:ND], comb[:, :, :], f32(chi[:, :, :]), ALU.subtract).then_inc(s_comb, 1)

            def comb_rows(b):
                dve.wait_ge(s_cT, b + 1)
                if b >= 2:
                    dve.wait_ge(s_C, (b - 1) * N_EXP)
                dve.tensor_copy(combT[b % 2][0:ND, :], pM[1][0:ND, 0:S]).then_inc(s_combT, 1)

            def weight_lo(e):
                dve.wait_ge(s_whi, e + 1)
                a, c = staged(e)
                dve.tensor_tensor(w13[1][:, e, :, :], a, f32(w13[0][:, e, :, :]), ALU.subtract)
                dve.tensor_tensor(w2[1][:, e, :], c, f32(w2[0][:, e, :]), ALU.subtract).then_inc(s_wlo, 1)

            def finish(b):
                dve.wait_ge(s_y, (b + 1) * NX)
                for t in range(NT):
                    xt = x_in.tile(b)[:, t, :]
                    last = dve.tensor_tensor(xt, pY[t][:, 0:D], xt, ALU.add)
                last.then_inc(s_yout, 1)

            prepare = {LN_AT: statistics, XN_AT: apply_norm, XT_AT: x_lo, CT_AT: comb_rows}
            prepare.update((RT_AT + n, f) for n, f in enumerate((biased_top, top_numbers, choose, weigh, split_weights)))
            dve.wait_ge(s_const, 3)
            dve.wait_ge(s_cst2, 1)
            dve.tensor_tensor(gw[1][:, :, :], gw_raw[:, :, :], f32(gw[0][:, :, :]), ALU.subtract).then_inc(s_cst2, 1)
            for at in sorted(prepare):
                prepare[at](0)
            weight_lo(0)
            weight_lo(1)
            for i, (b, e) in enumerate(XI):
                if b == 0 and e + 2 < NX:
                    weight_lo(e + 2)
                if e == W2_LAG - 1 and b:
                    finish(b - 1)
                dve.wait_ge(s_sig, i + 1)
                gu, h = pGU[i % 2], hid[i % 2]
                if i >= 2:
                    dve.wait_ge(s_hlo, i - 1)
                then(dve.tensor_tensor(h[:, :], gu[:, 0, :], sig[i % 2][:, :], ALU.mult))
                if e < N_EXP:
                    then(dve.tensor_tensor(h[:, :], gu[:, 1, :], h[:, :], ALU.mult))
                    dve.wait_ge(s_C, b * N_EXP + e + 1)
                    dve.tensor_tensor(h[:, :], pC[i % 2][:, 0:S], h[:, :], ALU.mult).then_inc(s_hid, 1)
                else:
                    dve.tensor_tensor(h[:, :], gu[:, 1, :], h[:, :], ALU.mult).then_inc(s_hid, 1)
                if e in prepare and b + 1 < B:
                    prepare[e](b + 1)
            finish(B - 1)


def program(nc, ins, out):
    x2 = nc.dram_tensor("x_plus_attention", ins["x"].shape, F32, kind="Internal").ap()
    attention_phase(nc, ins["ident"], ins["x"], ins["ctxT"], ins["mask"], ins["wqT"], ins["wkT"], ins["wvT"], ins["woT"], x2)
    expert_phase(nc, ins["ident"], ins["sel"], ins["iota"], x2, ins["gate_wT"], ins["gate_b"], ins["w13T"], ins["w2T"],
                 ins["w13_sT"], ins["w2_sT"], out)


def kernel(**inputs):
    import numpy as np
    import concourse.bacc as bacc
    from concourse.bass_utils import run_bass_kernel_spmd as run

    def laid_out(name, *axes):
        a = np.asarray(inputs[name])
        return np.ascontiguousarray(a.transpose(axes) if axes else a)

    arrays = {
        "x": laid_out("x"), "ctxT": laid_out("ctx_1024", 0, 2, 1), "mask": laid_out("fside_Bx1xSxS2_0"),
        "wqT": laid_out("L0_xattn_Wq", 1, 0), "wkT": laid_out("L0_xattn_Wk", 1, 0),
        "wvT": laid_out("L0_xattn_Wv", 1, 0), "woT": laid_out("L0_xattn_Wo", 1, 0),
        "gate_wT": laid_out("L0_ffn_gate_w", 1, 0), "gate_b": laid_out("L0_ffn_gate_b"),
        "w13T": laid_out("L0_ffn_w13", 0, 2, 1), "w2T": laid_out("L0_ffn_w2", 0, 2, 1),
        "w13_sT": laid_out("L0_ffn_w13_s", 1, 0), "w2_sT": laid_out("L0_ffn_w2_s", 1, 0),
    }
    n_exp, tiles = arrays["gate_wT"].shape[1], arrays["x"].shape[1] // P
    sel = np.zeros((P, n_exp, P), np.float32)
    for e in range(n_exp):
        sel[[e, n_exp + e], e, :] = 1.0
    arrays["ident"] = np.eye(P, dtype=np.float32)
    arrays["sel"] = sel
    arrays["iota"] = np.ascontiguousarray(np.broadcast_to(np.arange(n_exp, dtype=np.float32), (P, tiles, TOPK, n_exp)))

    nc = bacc.Bacc("TRN2", target_bir_lowering=False, num_devices=1)
    ins = {n: nc.dram_tensor(f"in_{n}", a.shape, mybir.dt.from_np(a.dtype), kind="ExternalInput").ap()
           for n, a in arrays.items()}
    out = nc.dram_tensor("out", arrays["x"].shape, F32, kind="ExternalOutput").ap()
    program(nc, ins, out)
    r = run(nc, [{f"in_{n}": a for n, a in arrays.items()}], core_ids=[0])
    return r.results[0]["out"]
```

```python
from contextlib import ExitStack

import concourse.bass as bass
from concourse import mybir

F32 = mybir.dt.float32
F32R = mybir.dt.float32r
U32 = mybir.dt.uint32
ALU = mybir.AluOpType
ACT = mybir.ActivationFunctionType
AXX = mybir.AxisListType.X

P = 128
EPS = 1e-5
TOPK = 4
ROUTE_SCALE = 2.5
BIG = 3.0e38
DMA = 16


class Ring:

    def __init__(self, make_tensor, make_sem, name, size, shape, dt):
        self.tiles = [make_tensor(f"{name}{i}", shape, dt) for i in range(size)]
        self.sems = [make_sem(f"s_{name}{i}") for i in range(size)]
        self.size = size

    def tile(self, n):
        return self.tiles[n % self.size]

    def sem(self, n):
        return self.sems[n % self.size]

    def wait(self, eng, n):
        eng.wait_ge(self.sem(n), DMA * (n // self.size + 1))


def f32(ap):
    return ap.bitcast(F32)


def split_products(eng, out, left, right, first=True, last=True):
    eng.matmul(out, left[0], right[0], start=first, stop=False)
    eng.matmul(out, left[0], right[1], start=False, stop=False)
    return eng.matmul(out, left[1], right[0], start=False, stop=last)


class Shared:

    def __init__(self, ctx, nc, B, S, D, n_exp):
        def sb(name, shape, dt=F32):
            return ctx.enter_context(nc.sbuf_tensor(name, shape, dt))

        def sem(name):
            return ctx.enter_context(nc.semaphore(name))

        self.ident = sb("ident", [P, P])
        self.gate = sb("gate", [P, D // P, n_exp])
        self.gate_b = sb("gate_b", [P, n_exp])
        self.iota = sb("iota", [P, n_exp])
        self.rows = Ring(sb, sem, "rows", 3, [P, S // P, D], F32)
        self.s_ident, self.s_gate = sem("s_ident"), sem("s_gate")
        self.s_rows_out = [sem(f"s_rows_out{i}") for i in range(3)]
        self.ahead = min(2, B - 1)


def attention_phase(nc, shared, ident_dram, gate_wT, gate_b, iota, x, ctxT, mask, wqT, wkT, wvT, woT, x2):
    B, S, D = x.shape
    INNER = wqT.shape[1]
    DH = 64
    H = INNER // DH
    NT = S // P
    NK = D // P
    NP = H // 2
    NE = INNER // P
    G = B * H

    EXP_LAG, T_LAG, PV_LAG, SUM_LAG = 1, 3, 4, 5
    E_RING, PT_RING, QK_RING = 5, 3, 3
    QK_LEAD = QK_RING - 1
    CM_STEP, CS_STEP = 1, 3
    WO_STEPS = (14, H, H + 6, H + 8)
    LN_STEP, XN_STEP, XT_STEP = 4, 6, 8
    V_STEPS = (10 - H, 12 - H, 2, 4)

    with ExitStack() as ctx:
        def sb(name, shape, dt=F32):
            return ctx.enter_context(nc.sbuf_tensor(name, shape, dt))

        def sem(name):
            return ctx.enter_context(nc.semaphore(name))

        def pair_of(name, shape):
            return sb(name + "_hi", shape, F32R), sb(name + "_lo", shape, F32R)

        wq, wk, wv = (pair_of(n, [P, NK, INNER]) for n in ("wq", "wk", "wv"))
        wo = pair_of("wo", [P, NE, D])
        CW = NT * S
        chunks = [(w[k * P:(k + 1) * P, c:c + CW], [part[:, k, c:c + CW] for part in parts])
                  for w, parts in ((wkT, wk), (wqT, wq), (wvT, wv)) for k in range(NK) for c in range(0, INNER, CW)]
        EC = CW // D
        chunks += [(woT[c * P:(c + EC) * P, :].rearrange("(k p) n -> p k n", p=P), [part[:, c:c + EC, :] for part in wo])
                   for c in range(0, NE, EC)]
        W_K = NK * INNER // CW
        W_Q, W_V, W_O = 2 * W_K, 3 * W_K, len(chunks)

        ident = shared.ident
        x_in = Ring(sb, sem, "x_in", 3, [P, NT, D], F32)
        c_in = Ring(sb, sem, "c_in", 2, [P, NK, S], F32)
        m_in = Ring(sb, sem, "m_in", 2, [P, NT, S], F32)
        s_x2out = shared.s_rows_out
        assert len(s_x2out) == x_in.size
        xn = shared.rows.tile(2)
        xnT = [pair_of(f"xnT{i}", [P, NK, S]) for i in range(2)]
        cT = [pair_of(f"cT{i}", [P, NK, S]) for i in range(2)]
        V = [sb(f"V{i}", [P, NT, NP, 4, DH], F32R) for i in range(2)]
        att = pair_of("att", [P, NE, S])
        att_sum = [sb(f"att_sum{i}", [P, S]) for i in range(2)]
        q_st = [sb(f"q_st{i}", [P, 2, S], F32R) for i in range(QK_RING)]
        k_st = [sb(f"k_st{i}", [P, 2, 2, S], F32R) for i in range(2)]
        k_sp = [sb(f"k_sp{i}", [P, 2, S], F32R) for i in range(2)]
        s_kdup = [sem(f"s_kdup{i}") for i in range(2)]
        E = [sb(f"E{i}", [P, NT, S]) for i in range(E_RING)]
        PT = [pair_of(f"PT{i}", [P, NT, S]) for i in range(PT_RING)]
        ways = shared.rows.tiles[:2] + x_in.tiles[:0:-1] + E + [c_in.tiles[1], m_in.tiles[1]]
        ways += ways[:3] + ways[:2]
        left_by = {11: 0, 12: 1, 13: 2, 14: 11}
        assert len(ways) == W_O

        def staged(i):
            buf = ways[i][:, :, :]
            return buf.rearrange("p a b -> p (a b)") if i < W_V else buf

        negmax = sb("negmax", [P, E_RING, NT])
        rowsum = sb("rowsum", [P, E_RING, NT])
        rinv = sb("rinv", [P, E_RING, NT])
        st6 = sb("st6", [P, NT, 6])
        mv = sb("mv", [P, NT, 2])
        veps = sb("veps", [P, NT])
        rstd = sb("rstd", [P, NT])
        mhalf = sb("mhalf", [P, NT])

        pj = [ctx.enter_context(nc.psum_tensor(f"pj{i}", [P, 512], F32)) for i in range(2)]
        pS = [ctx.enter_context(nc.psum_tensor(f"pS{i}", [P, NT, S], F32)) for i in range(2)]
        pT = [ctx.enter_context(nc.psum_tensor(f"pT{i}", [P, NT, S], F32)) for i in range(2)]
        pV = [ctx.enter_context(nc.psum_tensor(f"pV{i}", [P, 512], F32)) for i in range(2)]

        s_whi, s_wlo = sem("s_whi"), sem("s_wlo")
        s_olo, s_small, s_sum = sem("s_olo"), sem("s_small"), sem("s_sum")
        s_stage = [sem(f"s_stage{i}") for i in range(W_O)]
        s_const = sem("s_const")
        s_pj, s_hi, s_pjfree = sem("s_pj"), sem("s_hi"), sem("s_pjfree")
        s_S, s_T, s_PV = sem("s_S"), sem("s_T"), sem("s_PV")
        s_max, s_exp, s_rinv, s_norm = sem("s_max"), sem("s_exp"), sem("s_rinv"), sem("s_norm")
        s_pthi, s_ptlo, s_atthi, s_attlo = sem("s_pthi"), sem("s_ptlo"), sem("s_atthi"), sem("s_attlo")
        s_bn, s_agg, s_veps, s_rstd, s_xn = sem("s_bn"), sem("s_agg"), sem("s_veps"), sem("s_rstd"), sem("s_xn")
        s_chi, s_clo = sem("s_chi"), sem("s_clo")

        uses, number = {}, {}

        def use(step, what):
            number[what] = len(number)
            uses.setdefault(step, []).append(what)

        FIRST = -1
        for what in [("xT", 0)] + [(kind, pair) for kind in "kq" for pair in range(QK_LEAD)]:
            use(FIRST, what)
        for g in range(G - H + WO_STEPS[-1] + 1):
            b, h = divmod(g, H)
            if g < G and g // 2 + QK_LEAD < G // 2:
                use(g, ("kq"[g % 2], g // 2 + QK_LEAD))
            for part, at in enumerate(WO_STEPS):
                n, late = divmod(g - at, H)
                if late == 0 and 0 <= n < B:
                    use(g, ("wo", n, part))
            if h == XT_STEP and b + 1 < B:
                use(g, ("xT", b + 1))
            for part, at in enumerate(V_STEPS):
                n, late = divmod(g - at, H)
                if late == 0 and n < B and (n or at >= 0):
                    use(g, ("v", n, part))
                if g == part and at < 0:
                    use(g, ("v", 0, part))
        steps = range(max(uses) + 1)

        def start_up(weight, part):
            first = uses[FIRST]
            for i in range(W_K):
                weight(i)
            part(first[0])
            for i in range(W_K, W_Q):
                weight(i)
            for what in first[1:1 + QK_LEAD]:
                part(what)
            for i in range(W_Q, W_V):
                weight(i)
            for what in first[1 + QK_LEAD:]:
                part(what)


        WO_LAST = 2 * NT - 1
        assert len(V_STEPS) == 2 * NT == len(WO_STEPS)

        def qk_buf(pair):
            return pair % QK_RING

        def half(a):
            return slice(a * DH, (a + 1) * DH)

        def keys_here(eng, pair):
            eng.wait_ge(s_kdup[pair % 2], 4 * DMA * (pair // 2 + 1))

        block = ctx.enter_context(nc.Block())

        @block.sync
        def _(sp):

            def load_x(n):
                if n < B:
                    if n >= x_in.size:
                        sp.wait_ge(s_x2out[n % x_in.size], DMA * (n // x_in.size))
                    sp.dma_start(x_in.tile(n)[:, :, :], x[n].rearrange("(t p) d -> p t d", p=P)).then_inc(x_in.sem(n), DMA)

            def load_context(n):
                if n < B:
                    if n >= c_in.size:
                        sp.wait_ge(s_clo, n - c_in.size + 1)
                    sp.dma_start(c_in.tile(n)[:, :, :], ctxT[n].rearrange("(k p) s -> p k s", p=P)).then_inc(c_in.sem(n), DMA)

            def load_mask(n):
                if n < B:
                    if n >= 2:
                        sp.wait_ge(s_max, H * (n - 1))
                    sp.dma_start(m_in.tile(n)[:, :, :], mask[n, 0].rearrange("(t p) s -> p t s", p=P)).then_inc(m_in.sem(n), DMA)

            def load_weights(i):
                if i in left_by:
                    sp.wait_ge(s_wlo, left_by[i] + 1)
                if i == 15:
                    sp.wait_ge(s_olo, 1)
                sp.dma_start(staged(i), chunks[i][0]).then_inc(s_stage[i], DMA)

            def copy_keys(pair):
                sp.wait_ge(s_pjfree, number[("k", pair)] + 1)
                if pair >= 2:
                    sp.wait_ge(s_S, 2 * (pair - 1))
                for half in range(2):
                    for a in range(2):
                        sp.dma_start(f32(k_st[pair % 2][half * DH:(half + 1) * DH, a, :, :]),
                                     f32(k_sp[pair % 2][a * DH:(a + 1) * DH, :, :])).then_inc(s_kdup[pair % 2], DMA)

            def store(b):
                sp.wait_ge(s_pjfree, number[("wo", b, WO_LAST)] + 1)
                sp.dma_start(x2[b].rearrange("(t p) d -> p t d", p=P), x_in.tile(b)[:, :, :]).then_inc(
                    s_x2out[b % x_in.size], DMA)

            load_x(0)
            load_context(0)
            sp.dma_start(ident[:, :], ident_dram).then_inc(shared.s_ident, DMA)
            for i in range(W_Q):
                load_weights(i)
            load_mask(0)
            for i in range(W_Q, W_V):
                load_weights(i)
            for pair in range(QK_LEAD):
                copy_keys(pair)
            for i in range(W_V, W_O - 1):
                load_weights(i)
            sp.wait_ge(s_wlo, W_V)
            load_x(1)
            sp.dma_start(shared.gate[:, :, :], gate_wT.rearrange("(k p) e -> p k e", p=P)).then_inc(shared.s_gate, DMA)
            sp.dma_start(shared.gate_b[:, :], gate_b.partition_broadcast(P)).then_inc(shared.s_gate, DMA)
            sp.dma_start(shared.iota[:, :], iota).then_inc(shared.s_gate, DMA)

            for g in steps:
                b, h = divmod(g, H)
                for what in uses.get(g, ()):
                    if what[0] == "k":
                        copy_keys(what[1])
                if g == 1:
                    load_weights(W_O - 1)
                if g == W_O - W_V:
                    sp.wait_ge(s_olo, W_O - W_V)
                    load_x(2)
                if g == G - 1:
                    for n in range(shared.ahead):
                        sp.wait_ge(s_x2out[n % x_in.size], DMA * (n // x_in.size + 1))
                        sp.dma_start(shared.rows.tile(n)[:, :, :], x2[n].rearrange("(t p) d -> p t d", p=P)).then_inc(
                            shared.rows.sem(n), DMA)
                if h == CM_STEP:
                    load_context(b + 1)
                    load_mask(b + 1)
                if h == WO_STEPS[-1] - H and b:
                    store(b - 1)
                    load_x(b - 1 + x_in.size)

        @block.gpsimd
        def _(pool):
            pool.memset(mhalf[:, :], -0.5).then_inc(s_const, 1)
            pool.wait_ge(s_const, 1)

            def split_context(b):
                if b >= 2:
                    pool.wait_ge(s_pj, max(number[("k", b * NP - NP - 1)], number[("v", b - 2, 2 * NT - 1)]) + 1)
                c_in.wait(pool, b)
                hi, lo = cT[b % 2]
                pool.tensor_copy(hi[:, :, :], c_in.tile(b)[:, :, :]).then_inc(s_chi, 1)
                pool.wait_ge(s_chi, b + 1)
                pool.tensor_tensor(lo[:, :, :], c_in.tile(b)[:, :, :], f32(hi[:, :, :]), ALU.subtract).then_inc(s_clo, 1)

            def att_lo(pair):
                pool.wait_ge(s_atthi, pair + 1)
                j = pair % NP
                pool.tensor_tensor(att[1][:, j, :], att_sum[pair % 2][:, :], f32(att[0][:, j, :]), ALU.subtract).then_inc(s_attlo, 1)

            def inverse_std(b):
                pool.wait_ge(s_veps, b + 1)
                pool.tensor_tensor(rstd[:, :], veps[:, :], mhalf[:, :], ALU.pow).then_inc(s_rstd, 1)

            inverse_std(0)
            split_context(0)
            for g in range(G):
                b, h = divmod(g, H)
                if W_V + g < W_O:
                    hi, lo = chunks[W_V + g][1]
                    pool.wait_ge(s_whi, W_V + g + 1)
                    pool.tensor_tensor(lo, staged(W_V + g), f32(hi), ALU.subtract).then_inc(s_olo, 1)
                n = g - SUM_LAG
                if n >= 0 and n % 2:
                    att_lo(n // 2)
                pool.wait_ge(s_exp, g + 1)
                pool.wait_ge(s_rinv, g + 1)
                e, r = E[g % E_RING], g % E_RING
                for t in range(NT):
                    last = pool.tensor_scalar(e[:, t, :], e[:, t, :], rinv[:, r, t:t + 1], 1.0, ALU.mult, ALU.mult)
                last.then_inc(s_norm, 1)
                if h == CS_STEP and b + 1 < B:
                    split_context(b + 1)
                if h == LN_STEP and b + 1 < B:
                    inverse_std(b + 1)
            for pair in range((G - SUM_LAG) // 2, G // 2):
                att_lo(pair)

        @block.tensor
        def _(pe):
            def bank(what):
                n = number[what]
                if n >= 2:
                    pe.wait_ge(s_pjfree, n - 1)
                return pj[n % 2]

            def fill(what):
                kind, n = what[0], what[1]
                ps = bank(what)
                if kind == "xT":
                    pe.wait_ge(s_xn, n + 1)
                    for t in range(NT):
                        for k in range(NK):
                            last = pe.transpose(ps[:, k * S + t * P:k * S + (t + 1) * P],
                                                xn[:, t, k * P:(k + 1) * P], ident[:, :])
                elif kind == "v":
                    pe.wait_ge(s_clo, n + 1)
                    if n == 0:
                        pe.wait_ge(s_wlo, W_V)
                    half_at, t = divmod(what[2], NT)
                    for k in range(NK):
                        last = split_products(
                            pe, ps[:, :], [c[:, k, t * P:(t + 1) * P] for c in cT[n % 2]],
                            [w[:, k, half_at * 512:(half_at + 1) * 512] for w in wv], k == 0, k == NK - 1)
                elif kind == "q":
                    b, j = divmod(n, NP)
                    if n == 0:
                        pe.wait_ge(s_wlo, W_Q)
                    pe.wait_ge(s_pjfree, number[("xT", b)] + 1)
                    for k in range(NK):
                        last = split_products(
                            pe, ps[:, 0:S], [w[:, k, j * P:(j + 1) * P] for w in wq],
                            [a[:, k, :] for a in xnT[b % 2]], k == 0, k == NK - 1)
                elif kind == "k":
                    b, j = divmod(n, NP)
                    if n == 0:
                        pe.wait_ge(s_wlo, W_K)
                    pe.wait_ge(s_clo, b + 1)
                    for k in range(NK):
                        last = split_products(
                            pe, ps[:, 0:S], [w[:, k, j * P:(j + 1) * P] for w in wk],
                            [c[:, k, :] for c in cT[b % 2]], k == 0, k == NK - 1)
                else:
                    if n == 0:
                        pe.wait_ge(s_olo, W_O - W_V)
                    half_at, t = divmod(what[2], NT)
                    first, end = half_at * NE // 2, (half_at + 1) * NE // 2
                    for k in range(first, end):
                        pe.wait_ge(s_attlo, n * NP + k + 1)
                        last = split_products(pe, ps[:, 0:D], [a[:, k, t * P:(t + 1) * P] for a in att],
                                              [w[:, k, :] for w in wo], k == first, k == end - 1)
                last.then_inc(s_pj, 1)

            def scores(g):
                pair, a = divmod(g, 2)
                if a == 0:
                    pe.wait_ge(s_pjfree, number[("q", pair)] + 1)
                    keys_here(pe, pair)
                if g >= 2:
                    pe.wait_ge(s_max, g - 1)
                q = q_st[qk_buf(pair)]
                for t in range(NT):
                    left = q[:, a, t * P:(t + 1) * P]
                    pe.matmul(pS[g % 2][:, t, :], left, k_st[pair % 2][:, a, 0, :], start=True, stop=False)
                    last = pe.matmul(pS[g % 2][:, t, :], left, k_st[pair % 2][:, a, 1, :], start=False, stop=True)
                last.then_inc(s_S, 1)

            def transpose_probs(g):
                pe.wait_ge(s_norm, g + 1)
                if g >= 2:
                    pe.wait_ge(s_ptlo, g - 1)
                e = E[g % E_RING]
                for t in range(NT):
                    for k in range(NT):
                        last = pe.transpose(pT[g % 2][:, k, t * P:(t + 1) * P], e[:, t, k * P:(k + 1) * P], ident[:, :])
                last.then_inc(s_T, 1)

            def values(g):
                pair, a = divmod(g, 2)
                b, j = divmod(pair, NP)
                pe.wait_ge(s_ptlo, g + 1)
                if a == 0 and j % (NP // 2) == 0:
                    pe.wait_ge(s_pjfree, number[("v", b, NT - 1 if j == 0 else 2 * NT - 1)] + 1)
                if g >= 2:
                    pe.wait_ge(s_sum, g - 1)
                for k in range(NT):
                    for part in range(2):
                        last = pe.matmul(pV[g % 2][:, 0:S], V[b % 2][:, k, j, 2 * a:2 * a + 2, :],
                                         PT[g % PT_RING][part][:, k, :], start=k + part == 0, stop=k == NT - 1 and part == 1)
                last.then_inc(s_PV, 1)

            pe.wait_ge(shared.s_ident, DMA)
            for what in uses[FIRST]:
                fill(what)
            for g in steps:
                if 0 <= g < G:
                    scores(g)
                todo = uses.get(g, ())
                for what in todo[:1]:
                    fill(what)
                if 0 <= g - T_LAG < G:
                    transpose_probs(g - T_LAG)
                for what in todo[1:2]:
                    fill(what)
                if 0 <= g - PV_LAG < G:
                    values(g - PV_LAG)
                for what in todo[2:]:
                    fill(what)

        @block.scalar
        def _(act):
            def weight_hi(i):
                act.wait_ge(s_stage[i], DMA)
                act.activation(chunks[i][1][0], staged(i), ACT.Copy).then_inc(s_whi, 1)

            def hi_part(what):
                kind, n = what[0], what[1]
                if kind == "wo":
                    return
                act.wait_ge(s_pj, number[what] + 1)
                ps = pj[number[what] % 2]
                if kind == "xT":
                    if n >= 2:
                        act.wait_ge(s_pj, number[("q", (n - 1) * NP - 1)] + 1)
                    last = act.activation(xnT[n % 2][0][:, :, :], ps[:, :].rearrange("p (k s) -> p k s", k=NK), ACT.Copy)
                elif kind == "v":
                    if n >= 2 and what[2] == 0:
                        act.wait_ge(s_PV, (n - 1) * H)
                    half_at, t = divmod(what[2], NT)
                    j = half_at * NP // 2
                    last = act.activation(V[n % 2][:, t, j:j + NP // 2, 0:4:3, :],
                                          ps[:, :].rearrange("p (j a d) -> p j a d", a=2, d=DH), ACT.Copy)
                elif kind == "k":
                    if n >= 2:
                        keys_here(act, n - 2)
                    last = act.activation(k_sp[n % 2][:, 0, :], ps[:, 0:S], ACT.Copy)
                else:
                    if n >= QK_RING:
                        act.wait_ge(s_S, 2 * (n - QK_RING + 1))
                    for a in range(2):
                        at = slice(a * DH, (a + 1) * DH)
                        last = act.activation(q_st[qk_buf(n)][at, a, :], ps[at, 0:S], ACT.Copy)
                last.then_inc(s_hi, 1)

            start_up(weight_hi, hi_part)
            for g in steps:
                if W_V + g < W_O:
                    weight_hi(W_V + g)
                n = g - EXP_LAG
                if 0 <= n < G:
                    act.wait_ge(s_max, n + 1)
                    if n >= E_RING:
                        act.wait_ge(s_rinv, n - E_RING + 1)
                    r = n % E_RING
                    for t in range(NT):
                        last = act.activation(E[r][:, t, :], E[r][:, t, :], ACT.Exp, bias=negmax[:, r, t:t + 1],
                                              scale=-1.0, accum_out=rowsum[:, r, t:t + 1])
                    last.then_inc(s_exp, 1)
                n = g - SUM_LAG
                if 0 <= n < G:
                    pair, a = divmod(n, 2)
                    act.wait_ge(s_PV, n + 1)
                    if pair >= 2:
                        act.wait_ge(s_attlo, pair - 1)
                    act.activation(att_sum[pair % 2][half(a), :], pV[n % 2][half(1 - a), 0:S], ACT.Copy).then_inc(s_small, 1)
                todo = uses.get(g, ())
                for what in todo[:1]:
                    hi_part(what)
                m = g - T_LAG
                if 0 <= m < G:
                    act.wait_ge(s_T, m + 1)
                    if m >= PT_RING:
                        act.wait_ge(s_PV, m - PT_RING + 1)
                    act.activation(PT[m % PT_RING][0][:, :, :], pT[m % 2][:, :, :], ACT.Copy).then_inc(s_pthi, 1)
                for what in todo[1:2]:
                    hi_part(what)
                for what in todo[2:]:
                    hi_part(what)
                if 0 <= n < G and n % 2:
                    pair = n // 2
                    b, j = divmod(pair, NP)
                    act.wait_ge(s_sum, n + 1)
                    if b and j % (NP // 2) == 0:
                        act.wait_ge(s_pj, number[("wo", b - 1, NT - 1 if j == 0 else WO_LAST)] + 1)
                    act.activation(att[0][:, j, :], att_sum[pair % 2][:, :], ACT.Copy).then_inc(s_atthi, 1)

        @block.vector
        def _(dve):
            his = [0]

            def normalise(b):
                x_in.wait(dve, b)
                xb = x_in.tile(b)
                for t in range(NT):
                    last = dve.bn_stats(st6[:, t, :], xb[:, t, :])
                last.then_inc(s_bn, 1)
                dve.wait_ge(s_bn, b + 1)
                for t in range(NT):
                    last = dve.bn_aggr(mv[:, t, :], st6[:, t, :])
                last.then_inc(s_agg, 1)
                dve.wait_ge(s_agg, b + 1)
                dve.tensor_scalar(veps[:, :], mv[:, :, 1], EPS, None, ALU.add).then_inc(s_veps, 1)

            def apply_norm(b):
                dve.wait_ge(s_rstd, b + 1)
                if b:
                    dve.wait_ge(s_pj, number[("xT", b - 1)] + 1)
                for t in range(NT):
                    last = dve.tensor_scalar(xn[:, t, :], x_in.tile(b)[:, t, :], mv[:, t, 0:1], rstd[:, t:t + 1],
                                             ALU.subtract, ALU.mult)
                last.then_inc(s_xn, 1)

            def lo_part(what):
                kind, n = what[0], what[1]
                ps = pj[number[what] % 2]
                if kind == "wo":
                    dve.wait_ge(s_pj, number[what] + 1)
                    half_at, t = divmod(what[2], NT)
                    if half_at:
                        dve.wait_ge(s_pjfree, number[("wo", n, t)] + 1)
                    xt = x_in.tile(n)[:, t, :]
                    last = dve.tensor_tensor(xt, ps[:, 0:D], xt, ALU.add)
                    last.then_inc(s_pjfree, 1)
                    return
                his[0] += 1
                dve.wait_ge(s_hi, his[0])
                if kind == "xT":
                    hi, lo = xnT[n % 2]
                    last = dve.tensor_tensor(lo[:, :, :], ps[:, :].rearrange("p (k s) -> p k s", k=NK), f32(hi[:, :, :]), ALU.subtract)
                elif kind == "v":
                    half_at, t = divmod(what[2], NT)
                    j = half_at * NP // 2
                    hi, lo = (V[n % 2][:, t, j:j + NP // 2, at, :] for at in (slice(0, 4, 3), slice(1, 3)))
                    last = dve.tensor_tensor(lo, ps[:, :].rearrange("p (j a d) -> p j a d", a=2, d=DH), f32(hi), ALU.subtract)
                elif kind == "q":
                    q = q_st[qk_buf(n)]
                    dve.tensor_tensor(q[DH:P, 0, :], ps[0:DH, 0:S], f32(q[0:DH, 0, :]), ALU.subtract)
                    last = dve.tensor_tensor(q[0:DH, 1, :], ps[DH:P, 0:S], f32(q[DH:P, 1, :]), ALU.subtract)
                else:
                    last = dve.tensor_tensor(k_sp[n % 2][:, 1, :], ps[:, 0:S], f32(k_sp[n % 2][:, 0, :]), ALU.subtract)
                last.then_inc(s_pjfree, 1)

            def inverse_sums(g):
                r = g % E_RING
                dve.wait_ge(s_exp, g + 1)
                if g >= E_RING:
                    dve.wait_ge(s_norm, g - E_RING + 1)
                dve.reciprocal(rinv[:, r, :], rowsum[:, r, :]).then_inc(s_rinv, 1)

            def weight_lo(i):
                hi, lo = chunks[i][1]
                dve.wait_ge(s_whi, i + 1)
                dve.tensor_tensor(lo, staged(i), f32(hi), ALU.subtract).then_inc(s_wlo, 1)

            normalise(0)
            apply_norm(0)
            start_up(weight_lo, lo_part)
            for g in steps:
                b, h = divmod(g, H)
                if 0 <= g < G:
                    r = g % E_RING
                    dve.wait_ge(s_S, g + 1)
                    if g == 0:
                        dve.wait_ge(s_wlo, W_V)
                    if h == 0:
                        m_in.wait(dve, b)
                    if g >= E_RING:
                        dve.wait_ge(s_T, g - E_RING + 1)
                    for t in range(NT):
                        last = dve.tensor_tensor_reduce(
                            out=E[r][:, t, :], in0=pS[g % 2][:, t, :], in1=m_in.tile(b)[:, t, :], scale=-1.0,
                            scalar=BIG, op0=ALU.add, op1=ALU.min, accum_out=negmax[:, r, t:t + 1])
                    last.then_inc(s_max, 1)
                if 0 <= g - EXP_LAG < G:
                    inverse_sums(g - EXP_LAG)
                n = g - SUM_LAG
                if 0 <= n < G:
                    pair, a = divmod(n, 2)
                    dve.wait_ge(s_small, n + 1)
                    dve.tensor_tensor(att_sum[pair % 2][half(a), :], pV[n % 2][half(a), 0:S],
                                      att_sum[pair % 2][half(a), :], ALU.add).then_inc(s_sum, 1)
                todo = uses.get(g, ())
                for what in todo[:1]:
                    lo_part(what)
                if 0 <= g - T_LAG < G:
                    n = g - T_LAG
                    dve.wait_ge(s_pthi, n + 1)
                    hi, lo = PT[n % PT_RING]
                    dve.tensor_tensor(lo[:, :, :], pT[n % 2][:, :, :], f32(hi[:, :, :]), ALU.subtract).then_inc(s_ptlo, 1)
                for what in todo[1:2]:
                    lo_part(what)
                for what in todo[2:]:
                    lo_part(what)
                if 0 <= g < G and b + 1 < B:
                    if h == LN_STEP:
                        normalise(b + 1)
                    if h == XN_STEP:
                        apply_norm(b + 1)


def expert_phase(nc, shared, x2, comb_dram, w13T, w2T, w13_sT, w2_sT, out):
    B, S, D = x2.shape
    N_EXP = w13T.shape[0]
    INTER = w2T.shape[1]
    NX = N_EXP + 1
    NT, NK = S // P, D // P
    CB = 4

    with ExitStack() as ctx:
        def sb(name, shape, dt=F32):
            return ctx.enter_context(nc.sbuf_tensor(name, shape, dt))

        def sem(name):
            return ctx.enter_context(nc.semaphore(name))

        def pair_of(name, shape):
            return sb(name + "_hi", shape, F32R), sb(name + "_lo", shape, F32R)

        w13 = pair_of("w13", [P, NX, NK, 2 * INTER])
        w2 = pair_of("w2", [P, NX, D])
        gw = pair_of("gw", [P, NK, N_EXP])
        stage = Ring(sb, sem, "wstage", 8, [P, NK * 2 * INTER + D], F32)
        gw_raw, ident, x_in = shared.gate, shared.ident, shared.rows
        s_out = [sem(f"s_out{i}") for i in range(x_in.size)]
        xn = sb("xn2", [P, NT, D])
        xnT = [pair_of(f"xnT2_{i}", [P, NK, S]) for i in range(2)]
        st6, mv = sb("st6b", [P, NT, 6]), sb("mvb", [P, NT, 2])
        veps, rstd, mhalf = sb("vepsb", [P, NT]), sb("rstdb", [P, NT]), sb("mhalfb", [P, NT])
        lgT = sb("lgT", [N_EXP, S])
        sc, bi = sb("sc", [P, NT, N_EXP]), sb("bi", [P, NT, N_EXP])
        top, topi = sb("top", [P, NT, 8]), sb("topi", [P, NT, 8], U32)
        topf = sb("topf", [P, NT, TOPK])
        onehot = sb("onehot", [P, NT, TOPK, N_EXP])
        chosen, wsum, wrec = sb("chosen", [P, NT, N_EXP]), sb("wsum", [P, NT]), sb("wrec", [P, NT])
        wch, comb = sb("wch", [P, NT, N_EXP]), sb("comb", [P, NT, N_EXP])
        combT = [sb(f"combT{i}", [N_EXP, S]) for i in range(2)]
        comb_all = [sb(f"comb_all{i}", [P, N_EXP, S]) for i in range(2)]
        s_comb_out = sem("s_comb_out")
        s_comb_all = [[sem(f"s_comb_all{i}_{j}") for j in range(N_EXP // CB)] for i in range(2)]
        sig = [sb(f"sig{i}", [P, S]) for i in range(2)]
        hid = [sb(f"hid{i}", [P, S]) for i in range(2)]
        hsp = [pair_of(f"hsp{i}", [P, S]) for i in range(3)]

        pGU = [ctx.enter_context(nc.psum_tensor(f"pGU{i}", [P, 2, S], F32)) for i in range(2)]
        pY = [[ctx.enter_context(nc.psum_tensor(f"pY{i}_{t}", [P, 512], F32)) for t in range(NT)] for i in range(2)]
        pM = [ctx.enter_context(nc.psum_tensor(f"pM{i}", [P, 512], F32)) for i in range(2)]

        s_const, s_gw = sem("t_const"), sem("t_gw")
        s_whi, s_wlo, s_w2lo = sem("t_whi"), sem("t_wlo"), sem("t_w2lo")
        s_veps, s_rstd, s_xn = sem("t_veps"), sem("t_rstd"), sem("t_xn")
        s_xT, s_xhi, s_xlo = sem("t_xT"), sem("t_xhi"), sem("t_xlo")
        s_lg, s_lgc, s_lgt, s_sc = sem("t_lg"), sem("t_lgc"), sem("t_lgt"), sem("t_sc")
        s_comb, s_cT, s_combT = sem("t_comb"), sem("t_cT"), sem("t_combT")
        s_GU, s_sig, s_hid, s_hhi, s_hlo, s_y, s_yout = (
            sem(n) for n in ("t_GU", "t_sig", "t_hid", "t_hhi", "t_hlo", "t_y", "t_yout"))
        s_chain = sem("t_chain")

        XI = [(b, e) for b in range(B) for e in range(NX)]
        N = len(XI)
        W2_LAG = 2
        LN_AT, XN_AT, XT_AT, LG_AT, LGT_AT, RT_AT, CT_AT = 1, 2, 4, 5, 6, 7, 12
        END_AT = 3

        block = ctx.enter_context(nc.Block())

        @block.sync
        def _(sp):
            def load(n):
                if n < B:
                    if n >= 3:
                        sp.wait_ge(s_out[n % 3], DMA * (n // 3))
                    sp.wait_ge(shared.s_rows_out[n % 3], DMA * (n // 3 + 1))
                    sp.dma_start(x_in.tile(n)[:, :, :], x2[n].rearrange("(t p) d -> p t d", p=P)).then_inc(x_in.sem(n), DMA)

            for n in range(shared.ahead, 1):
                load(n)
            def spread(b):
                sp.wait_ge(s_combT, b + 1)
                sp.dma_start(comb_dram[b], combT[b % 2][:, :]).then_inc(s_comb_out, DMA)
                if b >= 2:
                    sp.wait_ge(s_hid, (b - 1) * NX)
                sp.wait_ge(s_comb_out, DMA * (b + 1))
                for j, arrived in enumerate(s_comb_all[b % 2]):
                    at = slice(j * CB, (j + 1) * CB)
                    sp.dma_start(comb_all[b % 2][:, at, :], comb_dram[b, at, :].partition_broadcast(P)).then_inc(arrived, DMA)

            W13 = NK * 2 * INTER
            for e in range(NX):
                if e == stage.size:
                    spread(0)
                if e >= stage.size:
                    sp.wait_ge(s_wlo, e - stage.size + 1)
                    sp.wait_ge(s_w2lo, e - stage.size + 1)
                a = w13T[e - 1] if e else w13_sT
                c = w2T[e - 1] if e else w2_sT
                sp.dma_start(stage.tile(e)[:, 0:W13].rearrange("p (k n) -> p k n", k=NK),
                             a.rearrange("(k p) n -> p k n", p=P)).then_inc(stage.sem(e), DMA)
                sp.dma_start(stage.tile(e)[:, W13:W13 + D], c).then_inc(stage.sem(e), DMA)
            for n in range(max(1, shared.ahead), x_in.size):
                load(n)

            def store(b):
                sp.wait_ge(s_yout, b + 1)
                sp.dma_start(out[b].rearrange("(t p) d -> p t d", p=P), x_in.tile(b)[:, :, :]).then_inc(s_out[b % 3], DMA)

            for b in range(B):
                if b:
                    store(b - 1)
                    load(b + 2)
                if b + 1 < B:
                    spread(b + 1)
            store(B - 1)
            for b in range(max(0, B - 3), B):
                sp.wait_ge(s_out[b % 3], DMA * (b // 3 + 1))

        def weights_here(eng, e):
            eng.wait_ge(stage.sem(e), 2 * DMA * (e // stage.size + 1))

        def staged(e):
            W13 = NK * 2 * INTER
            t = stage.tile(e)
            return t[:, 0:W13].rearrange("p (k n) -> p k n", k=NK), t[:, W13:W13 + D]

        @block.gpsimd
        def _(pool):
            pool.memset(mhalf[:, :], -0.5).then_inc(s_const, 1)
            pool.wait_ge(s_const, 1)

            def inverse_std(b):
                pool.wait_ge(s_veps, b + 1)
                pool.tensor_tensor(rstd[:, :], veps[:, :], mhalf[:, :], ALU.pow).then_inc(s_rstd, 1)

            inverse_std(0)
            for i, (b, e) in enumerate(XI):
                if b == 0:
                    pool.wait_ge(s_whi, e + 1)
                    _, c = staged(e)
                    pool.tensor_tensor(w2[1][:, e, :], c, f32(w2[0][:, e, :]), ALU.subtract).then_inc(s_w2lo, 1)
                pool.wait_ge(s_hhi, i + 1)
                hi, lo = hsp[i % 3]
                if i >= 3:
                    pool.wait_ge(s_y, i - 2)
                pool.tensor_tensor(lo[:, :], hid[i % 2][:, :], f32(hi[:, :]), ALU.subtract).then_inc(s_hlo, 1)
                if e == LN_AT and b + 1 < B:
                    inverse_std(b + 1)

        @block.tensor
        def _(pe):
            def transposed_x(b):
                pe.wait_ge(s_xn, b + 1)
                for t in range(NT):
                    for k in range(NK):
                        last = pe.transpose(pM[0][:, k * S + t * P:k * S + (t + 1) * P],
                                            xn[:, t, k * P:(k + 1) * P], ident[:, :])
                last.then_inc(s_xT, 1)

            def logits(b):
                pe.wait_ge(s_xlo, b + 1)
                if b:
                    pe.wait_ge(s_combT, b)
                for k in range(NK):
                    last = split_products(pe, pM[1][0:N_EXP, 0:S], [g[:, k, :] for g in gw],
                                          [a[:, k, :] for a in xnT[b % 2]], k == 0, k == NK - 1)
                last.then_inc(s_lg, 1)

            def logits_by_token(b):
                pe.wait_ge(s_lgc, b + 1)
                for t in range(NT):
                    last = pe.transpose(pM[1][:, t * N_EXP:(t + 1) * N_EXP], lgT[:, t * P:(t + 1) * P],
                                        ident[0:N_EXP, 0:N_EXP])
                last.then_inc(s_lgt, 1)

            def comb_by_expert(b):
                pe.wait_ge(s_comb, b + 1)
                for t in range(NT):
                    last = pe.transpose(pM[1][0:N_EXP, t * P:(t + 1) * P], comb[:, t, :], ident[:, :])
                last.then_inc(s_cT, 1)

            prepare = {XT_AT: transposed_x, LG_AT: logits, LGT_AT: logits_by_token, CT_AT: comb_by_expert}
            transposed_x(0)
            pe.wait_ge(s_gw, 2)
            logits(0)
            logits_by_token(0)
            for i in range(N + W2_LAG):
                if i < N:
                    b, e = XI[i]
                    if b == 0:
                        pe.wait_ge(s_wlo, e + 1)
                    if i >= 2:
                        pe.wait_ge(s_hid, i - 1)
                    for m in range(2):
                        for k in range(NK):
                            last = split_products(pe, pGU[i % 2][:, m, :],
                                                  [w[:, e, k, m * INTER:(m + 1) * INTER] for w in w13],
                                                  [a[:, k, :] for a in xnT[b % 2]], k == 0, k == NK - 1)
                    last.then_inc(s_GU, 1)
                    if i == 0:
                        comb_by_expert(0)
                    if e in prepare and b + 1 < B:
                        prepare[e](b + 1)
                if i >= W2_LAG:
                    n = i - W2_LAG
                    b, e = XI[n]
                    pe.wait_ge(s_hlo, n + 1)
                    if b == 0:
                        pe.wait_ge(s_w2lo, e + 1)
                    if e == 0 and b >= 2:
                        pe.wait_ge(s_yout, b - 1)
                    for t in range(NT):
                        last = split_products(pe, pY[b % 2][t][:, 0:D], [h[:, t * P:(t + 1) * P] for h in hsp[n % 3]],
                                              [w[:, e, :] for w in w2], e == 0, e == NX - 1)
                    last.then_inc(s_y, 1)

        @block.scalar
        def _(act):
            act.wait_ge(shared.s_gate, 3 * DMA)
            act.activation(gw[0][:, :, :], gw_raw[:, :, :], ACT.Copy).then_inc(s_gw, 1)

            def x_hi(b):
                act.wait_ge(s_xT, b + 1)
                if b >= 2:
                    act.wait_ge(s_GU, (b - 1) * NX)
                act.activation(xnT[b % 2][0][:, :, :], pM[0][:, :].rearrange("p (k s) -> p k s", k=NK), ACT.Copy).then_inc(s_xhi, 1)

            def logit_copy(b):
                act.wait_ge(s_lg, b + 1)
                act.activation(lgT[:, :], pM[1][0:N_EXP, 0:S], ACT.Copy).then_inc(s_lgc, 1)

            def gate_scores(b):
                act.wait_ge(s_lgt, b + 1)
                if b:
                    act.wait_ge(s_comb, b)
                act.activation(sc[:, :, :], pM[1][:, 0:NT * N_EXP].rearrange("p (t e) -> p t e", t=NT),
                               ACT.Sigmoid).then_inc(s_sc, 1)

            def weight_hi(e):
                weights_here(act, e)
                a, c = staged(e)
                act.activation(w13[0][:, e, :, :], a, ACT.Copy)
                act.activation(w2[0][:, e, :], c, ACT.Copy).then_inc(s_whi, 1)

            def hidden_hi(i):
                act.wait_ge(s_hid, i + 1)
                if i >= 3:
                    act.wait_ge(s_y, i - 2)
                act.activation(hsp[i % 3][0][:, :], hid[i % 2][:, :], ACT.Copy).then_inc(s_hhi, 1)

            prepare = {XT_AT: x_hi, LG_AT: logit_copy, LGT_AT: gate_scores}
            weight_hi(0)
            for at in sorted(prepare):
                prepare[at](0)
            weight_hi(1)
            for i, (b, e) in enumerate(XI):
                if b == 0 and e + 2 < NX:
                    weight_hi(e + 2)
                act.wait_ge(s_GU, i + 1)
                if i >= 2:
                    act.wait_ge(s_hid, i - 1)
                act.activation(sig[i % 2][:, :], pGU[i % 2][:, 0, :], ACT.Sigmoid).then_inc(s_sig, 1)
                if e in prepare and b + 1 < B:
                    prepare[e](b + 1)
                if i:
                    hidden_hi(i - 1)
            hidden_hi(N - 1)

        @block.vector
        def _(dve):
            chain = [0]

            def then(ins):
                chain[0] += 1
                ins.then_inc(s_chain, 1)
                dve.wait_ge(s_chain, chain[0])

            def statistics(b):
                x_in.wait(dve, b)
                xb = x_in.tile(b)
                dve.bn_stats(st6[:, 0, :], xb[:, 0, :])
                then(dve.bn_stats(st6[:, 1, :], xb[:, 1, :]))
                dve.bn_aggr(mv[:, 0, :], st6[:, 0, :])
                then(dve.bn_aggr(mv[:, 1, :], st6[:, 1, :]))
                dve.tensor_scalar(veps[:, :], mv[:, :, 1], EPS, None, ALU.add).then_inc(s_veps, 1)

            def apply_norm(b):
                dve.wait_ge(s_rstd, b + 1)
                if b:
                    dve.wait_ge(s_xT, b)
                for t in range(NT):
                    last = dve.tensor_scalar(xn[:, t, :], x_in.tile(b)[:, t, :], mv[:, t, 0:1], rstd[:, t:t + 1],
                                             ALU.subtract, ALU.mult)
                last.then_inc(s_xn, 1)

            def x_lo(b):
                dve.wait_ge(s_xhi, b + 1)
                hi, lo = xnT[b % 2]
                dve.tensor_tensor(lo[:, :, :], pM[0][:, :].rearrange("p (k s) -> p k s", k=NK), f32(hi[:, :, :]),
                                  ALU.subtract).then_inc(s_xlo, 1)

            def biased_top(b):
                dve.wait_ge(s_sc, b + 1)
                then(dve.tensor_tensor(bi[:, :, :], sc[:, :, :], shared.gate_b[:, :].unsqueeze(1).broadcast_to([P, NT, N_EXP]),
                                       ALU.add))
                for t in range(NT):
                    last = dve.max(top[:, t, :], bi[:, t, :])
                then(last)

            def top_numbers(b):
                for t in range(NT):
                    last = dve.max_index(topi[:, t, :], top[:, t, :], bi[:, t, :])
                then(last)
                then(dve.tensor_copy(topf[:, :, :], topi[:, :, 0:TOPK]))

            def choose(b):
                then(dve.tensor_tensor(onehot[:, :, :, :],
                                       shared.iota[:, :].unsqueeze(1).unsqueeze(1).broadcast_to([P, NT, TOPK, N_EXP]),
                                       topf[:, :, :].unsqueeze(3).broadcast_to([P, NT, TOPK, N_EXP]), ALU.is_equal))
                then(dve.reduce_sum(chosen[:, :, :], onehot[:, :, :, :].rearrange("p t j e -> p t e j"), AXX))

            def weigh(b):
                then(dve.tensor_tensor(wch[:, :, :], chosen[:, :, :], sc[:, :, :], ALU.mult))
                then(dve.reduce_sum(wsum[:, :], wch[:, :, :], AXX))
                then(dve.reciprocal(wrec[:, :], wsum[:, :]))
                if b:
                    dve.wait_ge(s_cT, b)
                for t in range(NT):
                    last = dve.tensor_scalar(comb[:, t, :], wch[:, t, :], wrec[:, t:t + 1], ROUTE_SCALE, ALU.mult, ALU.mult)
                last.then_inc(s_comb, 1)

            def comb_rows(b):
                dve.wait_ge(s_cT, b + 1)
                if b >= 2:
                    dve.wait_ge(s_comb_out, DMA * (b - 1))
                dve.tensor_copy(combT[b % 2][:, :], pM[1][0:N_EXP, 0:S]).then_inc(s_combT, 1)

            def weight_lo(e):
                dve.wait_ge(s_whi, e + 1)
                a, _ = staged(e)
                dve.tensor_tensor(w13[1][:, e, :, :], a, f32(w13[0][:, e, :, :]), ALU.subtract).then_inc(s_wlo, 1)

            def finish(b):
                dve.wait_ge(s_y, (b + 1) * NX)
                for t in range(NT):
                    xt = x_in.tile(b)[:, t, :]
                    last = dve.tensor_tensor(xt, pY[b % 2][t][:, 0:D], xt, ALU.add)
                last.then_inc(s_yout, 1)

            prepare = {LN_AT: statistics, XN_AT: apply_norm, XT_AT: x_lo, CT_AT: comb_rows}
            prepare.update((RT_AT + n, f) for n, f in enumerate((biased_top, top_numbers, choose, weigh)))
            dve.wait_ge(s_gw, 1)
            dve.tensor_tensor(gw[1][:, :, :], gw_raw[:, :, :], f32(gw[0][:, :, :]), ALU.subtract).then_inc(s_gw, 1)
            for at in sorted(prepare):
                if at == XT_AT:
                    weight_lo(0)
                prepare[at](0)
            weight_lo(1)
            for i, (b, e) in enumerate(XI):
                if b == 0 and e + 2 < NX:
                    weight_lo(e + 2)
                if e == END_AT and b:
                    finish(b - 1)
                dve.wait_ge(s_sig, i + 1)
                gu, h = pGU[i % 2], hid[i % 2]
                if i >= 2:
                    dve.wait_ge(s_hlo, i - 1)
                then(dve.tensor_tensor(h[:, :], gu[:, 0, :], sig[i % 2][:, :], ALU.mult))
                if e:
                    then(dve.tensor_tensor(h[:, :], gu[:, 1, :], h[:, :], ALU.mult))
                    if (e - 1) % CB == 0:
                        dve.wait_ge(s_comb_all[b % 2][(e - 1) // CB], DMA * (b // 2 + 1))
                    dve.tensor_tensor(h[:, :], comb_all[b % 2][:, e - 1, :], h[:, :], ALU.mult).then_inc(s_hid, 1)
                else:
                    dve.tensor_tensor(h[:, :], gu[:, 1, :], h[:, :], ALU.mult).then_inc(s_hid, 1)
                if e in prepare and b + 1 < B:
                    prepare[e](b + 1)
            finish(B - 1)


def program(nc, ins, out):
    B, S, D = ins["x"].shape
    n_exp = ins["gate_wT"].shape[1]
    x2 = nc.dram_tensor("x_plus_attention", [B, S, D], F32, kind="Internal").ap()
    comb = nc.dram_tensor("combination_weights", [B, n_exp, S], F32, kind="Internal").ap()
    with ExitStack() as ctx:
        shared = Shared(ctx, nc, B, S, D, n_exp)
        attention_phase(nc, shared, ins["ident"], ins["gate_wT"], ins["gate_b"], ins["iota"], ins["x"], ins["ctxT"],
                        ins["mask"], ins["wqT"], ins["wkT"], ins["wvT"], ins["woT"], x2)
        expert_phase(nc, shared, x2, comb, ins["w13T"], ins["w2T"], ins["w13_sT"], ins["w2_sT"], out)


def kernel(**inputs):
    import numpy as np
    import concourse.bacc as bacc
    from concourse.bass_utils import run_bass_kernel_spmd as run

    def laid_out(name, *axes):
        a = np.asarray(inputs[name])
        return np.ascontiguousarray(a.transpose(axes) if axes else a)

    arrays = {
        "x": laid_out("x"), "ctxT": laid_out("ctx_1024", 0, 2, 1), "mask": laid_out("fside_Bx1xSxS2_0"),
        "wqT": laid_out("L0_xattn_Wq", 1, 0), "wkT": laid_out("L0_xattn_Wk", 1, 0),
        "wvT": laid_out("L0_xattn_Wv", 1, 0), "woT": laid_out("L0_xattn_Wo", 1, 0),
        "gate_wT": laid_out("L0_ffn_gate_w", 1, 0), "gate_b": laid_out("L0_ffn_gate_b"),
        "w13T": laid_out("L0_ffn_w13", 0, 2, 1), "w2T": laid_out("L0_ffn_w2", 0, 2, 1),
        "w13_sT": laid_out("L0_ffn_w13_s", 1, 0), "w2_sT": laid_out("L0_ffn_w2_s", 1, 0),
    }
    n_exp = arrays["gate_wT"].shape[1]
    arrays["ident"] = np.eye(P, dtype=np.float32)
    arrays["iota"] = np.ascontiguousarray(np.broadcast_to(np.arange(n_exp, dtype=np.float32), (P, n_exp)))

    nc = bacc.Bacc("TRN2", target_bir_lowering=False, num_devices=1)
    ins = {n: nc.dram_tensor(f"in_{n}", a.shape, mybir.dt.from_np(a.dtype), kind="ExternalInput").ap()
           for n, a in arrays.items()}
    out = nc.dram_tensor("out", arrays["x"].shape, F32, kind="ExternalOutput").ap()
    program(nc, ins, out)
    r = run(nc, [{f"in_{n}": a for n, a in arrays.items()}], core_ids=[0])
    return r.results[0]["out"]
```
